# Optimizing a Trainium2 kernel written in Bass

```python
import numpy as np
import jax
import jax.numpy as jnp

def _softmax(x, axis=-1):
    return jax.nn.softmax(x, axis=axis)

def _gelu(x):
    return jax.nn.gelu(x, approximate=True)

def _silu(x):
    return jax.nn.silu(x)

def _sigmoid(x):
    return jax.nn.sigmoid(x)

def _layernorm(x, axis=-1, eps=1e-05):
    m = jnp.mean(x, axis=axis, keepdims=True)
    v = jnp.var(x, axis=axis, keepdims=True)
    return (x - m) / jnp.sqrt(v + eps)

def _scatter_add(tgt, idx, src, axis=0):
    return tgt.at[idx].add(src)

def _segment_sum(src, seg, n):
    return jax.ops.segment_sum(src, seg, n)
kernel_name = 'mk_adj_resnorm_d1_adj_r2_0a16bd'

def setup_inputs(seed: int=0):
    np.random.seed(seed)
    _w = jnp.asarray

    def _rec_inputs():
        import jax
        import jax.numpy as jnp
        _gk = jax.random.key(seed)
        x = -0.000929 + 1 * jax.random.normal(jax.random.fold_in(_gk, 1), (2048, 256), jnp.float32)
        _w = (1.0 + jnp.arange(2048, dtype=jnp.float32)) ** (-0.5)
        _w = _w / _w.mean()
        _pij = jnp.clip(0.000976562 * _w[:, None] * _w[None, :], 0.0, 1.0)
        _a = jax.random.uniform(jax.random.fold_in(_gk, 2), (2048, 2048)) < _pij
        _af = _a.astype(jnp.float32)
        _af = _af * jax.random.uniform(jax.random.fold_in(_gk, 3), (2048, 2048), jnp.float32, 0.05, 5.22011)
        adj = _af
        return (x, adj)
    x, adj = _rec_inputs()

    def _L0_gnn_setup():
        import jax, jax.numpy as jnp
        import numpy as np
        N = 1024
        HID = 256
        H = 8
        key = jax.random.key(seed)
        ks = jax.random.split(key, 8)
        x = jax.random.normal(ks[0], (N, HID), dtype=jnp.float32)
        sp = jax.random.normal(ks[1], (N, N), dtype=jnp.float32)
        zero_mask = jax.random.uniform(ks[2], (N, N)) < 0.2
        spatial_encoding = jnp.where(zero_mask, 0.0, sp)
        edge_encoding = jax.random.normal(ks[3], (N, N), dtype=jnp.float32)
        s = 1.0 / np.sqrt(HID)
        Wq = jax.random.normal(ks[4], (HID, HID * H), dtype=jnp.float32) * s
        Wk = jax.random.normal(ks[5], (HID, HID * H), dtype=jnp.float32) * s
        Wv = jax.random.normal(ks[6], (HID, HID * H), dtype=jnp.float32) * s
        Wout = jax.random.normal(ks[7], (HID * H, HID), dtype=jnp.float32) * (1.0 / np.sqrt(HID * H))
        return {'x': x, 'spatial_encoding': spatial_encoding, 'edge_encoding': edge_encoding, 'Wq': Wq, 'Wk': Wk, 'Wv': Wv, 'Wout': Wout}
    _L0_gnn_all = _L0_gnn_setup()
    _L0_gnn_in = {k: v for k, v in _L0_gnn_all.items() if k in ('Wq', 'Wk', 'Wv', 'Wout')}
    del _L0_gnn_all
    return {'x': x, 'adj': adj, 'L0_gnn_Wq': _L0_gnn_in['Wq'], 'L0_gnn_Wk': _L0_gnn_in['Wk'], 'L0_gnn_Wv': _L0_gnn_in['Wv'], 'L0_gnn_Wout': _L0_gnn_in['Wout']}

def reference(x, adj, L0_gnn_Wq, L0_gnn_Wk, L0_gnn_Wv, L0_gnn_Wout):
    import jax
    import jax.numpy as jnp

    def _L0_gnn_ref(x, spatial_encoding, edge_encoding, Wq, Wk, Wv, Wout):
        import jax, jax.numpy as jnp
        import numpy as np
        N = 1024
        HID = 256
        H = 8
        n, d = x.shape
        h = Wq.shape[1] // d
        scale = d ** (-0.5)
        q = (x @ Wq).reshape(h, n, d)
        k = (x @ Wk).reshape(h, n, d)
        v = (x @ Wv).reshape(h, n, d)
        a = jnp.einsum('hnd,hmd->hnm', q, k) * scale
        a = a + spatial_encoding + edge_encoding
        mask = spatial_encoding == 0.0
        a = jnp.where(mask, -1000000.0, a)
        a = jax.nn.softmax(a, axis=-1)
        a = jnp.where(mask, 0.0, a)
        out = jnp.einsum('hnm,hmd->hnd', a, v)
        out = out.transpose(1, 0, 2).reshape(n, h * d)
        return out @ Wout
    x = _layernorm(x + _L0_gnn_ref(x, adj, adj, L0_gnn_Wq, L0_gnn_Wk, L0_gnn_Wv, L0_gnn_Wout), axis=-1)
    return x

_drawn_inputs = setup_inputs


def setup_inputs(seed=0):
    import zlib

    import numpy as np

    out = dict(_drawn_inputs(seed))
    spreads = {}
    factors = {}
    for name, (base, spread) in spreads.items():
        noise = np.random.default_rng([zlib.crc32(name.encode()), seed]).standard_normal(out[name].shape)
        drawn = base * np.exp(spread * noise) if base else spread * noise
        out[name] = jnp.asarray(drawn.astype(out[name].dtype))
    for name, factor in factors.items():
        out[name] = (out[name] * factor).astype(out[name].dtype)
    return out
```

```python
from contextlib import ExitStack

import numpy as np
import concourse.bass as bass
from concourse import mybir

ALU = mybir.AluOpType
ACT = mybir.ActivationFunctionType
AX = mybir.AxisListType
F32 = mybir.dt.float32
F32R = mybir.dt.float32r

P = 128
HIDDEN = 256
HEADS = 8
N = 2048
ROWS = N // HEADS
BLOCKS = N // ROWS
KC = HIDDEN // P
TILES = N // P
GROUP = 4
GROUPS = TILES // GROUP
GN = GROUP * P
BANK = 512
CHUNKS = N // BANK
HALF = N // 2
HJ = HALF // BLOCKS

EPS = 1e-5
MASKED = -1.0e6
BIG = -(2.0 ** 100)
NONE = -1.0e38
Q_SCALE = HIDDEN ** -0.5 / 2

RING = 6
X_USES = KC
K_AT = 0
Q0_AT = K_AT + BLOCKS
V_AT = Q0_AT + 2
G_AT = V_AT + BLOCKS
SCORES_AT, Q_AT, OUT_AT, PROBS_AT = [], [], [], []
_at = G_AT
for _g in range(GROUPS):
    SCORES_AT.append(_at)
    Q_AT.append(SCORES_AT[_g] + GROUP * CHUNKS)
    OUT_AT.append(Q_AT[_g] + (2 if _g < GROUPS - 1 else 0))
    PROBS_AT.append(OUT_AT[_g] + (2 if _g else 0))
    _at = PROBS_AT[_g] + TILES
X_AT = _at
OUT_LAST_AT = X_AT + X_USES
USES = OUT_LAST_AT + 2
assert USES % RING == 0

SPLIT_USES = [u for u in range(USES) if u < G_AT or X_AT <= u < OUT_LAST_AT
              or any(Q_AT[g] <= u < OUT_AT[g] or PROBS_AT[g] <= u < PROBS_AT[g] + TILES for g in range(GROUPS))]
SPLITS = len(SPLIT_USES)

UNITS = ([("k", c) for c in range(BLOCKS)] + [("q", c) for c in range(2)]
         + [("v", c) for c in range(BLOCKS)] + [("q", c) for c in range(2, BLOCKS)])
UNIT_USE = list(range(G_AT)) + [Q_AT[g] + b for g in range(GROUPS - 1) for b in range(2)]
NU = len(UNITS)
assert len(UNIT_USE) == NU
RAW = 3
SPLIT = 2
ADJ = 4
MASKS = 2
BIAS = 2
PT = 3
HALVES = 2 * TILES
assert NU % RAW == 0 and HALVES % ADJ == 0
FEED = ([("adj", k) for k in range(4)] + [("w", k) for k in range(G_AT)] + [("wout", 0)]
        + [("w", k) for k in range(18, 20)] + [("adj", k) for k in range(4, 12)]
        + [("w", k) for k in range(20, 22)] + [("adj", k) for k in range(12, 20)]
        + [("w", k) for k in range(22, 24)] + [("adj", k) for k in range(20, HALVES)])


def build(nc, x, adj, wq, wk, wv, wout, out):
    adj_rows = adj.rearrange("(s p c) m -> c s p m", p=P, c=BLOCKS)
    x_rows = x.rearrange("(s p c) d -> c p s d", p=P, c=BLOCKS)
    out_rows = out.rearrange("(s p c) d -> c p s d", p=P, c=BLOCKS)
    weights = {"q": wq, "k": wk, "v": wv}

    with ExitStack() as ctx:
        def sb(name, shape, dt=F32):
            return ctx.enter_context(nc.sbuf_tensor(name, shape, dt))

        def sem(name):
            return ctx.enter_context(nc.semaphore(name))

        kt = sb("kt", [P, 2, KC, N], F32R)
        vv = sb("vv", [P, 2, TILES, HIDDEN], F32R)
        qt = sb("qt", [P, 2, KC, GN], F32R)
        xt = sb("xt", [P, 2, KC, ROWS], F32R)
        pt = sb("pt", [P, PT, 2, GN], F32R)
        ot = sb("ot", [P, 2, KC, GN], F32R)
        w_split = sb("w_split", [P, SPLIT, 2, KC, HIDDEN], F32R)
        wout_split = sb("wout_split", [P, 2, KC, HIDDEN], F32R)
        w_raw = sb("w_raw", [P, RAW, KC, HIDDEN])
        wout_raw = sb("wout_raw", [P, KC, HIDDEN])
        x_raw = sb("x_raw", [P, ROWS // P, HIDDEN])
        adj_raw = sb("adj_raw", [P, ADJ, HALF])
        mask = sb("mask", [P, MASKS, HALF])
        bias = sb("bias", [P, BIAS, N])
        probs = sb("probs", [P, GROUP, N])
        y = sb("y", [P, TILES, HIDDEN])
        ident = sb("ident", [P, P])
        maxima = sb("maxima", [P, CHUNKS + 1])
        top = sb("top", [P, 1])
        unmasked = sb("unmasked", [P, 1])
        shift = sb("shift", [P, GROUP])
        masked_sum = sb("masked_sum", [P, TILES, 2])
        total_masked = sb("total_masked", [P, GROUP])
        exp_sum = sb("exp_sum", [P, GROUP])
        masked_arg = sb("masked_arg", [P, GROUP])
        masked_exp = sb("masked_exp", [P, GROUP])
        masked_part = sb("masked_part", [P, GROUP])
        denom = sb("denom", [P, GROUP])
        inv_denom = sb("inv_denom", [P, GROUP])
        stats = sb("stats", [P, TILES, 6])
        moments = sb("moments", [P, TILES, 2])
        var_eps = sb("var_eps", [P, TILES])
        std = sb("std", [P, TILES])
        inv_std = sb("inv_std", [P, TILES])

        ring = ctx.enter_context(nc.psum_tensor("ring", [P, RING, BANK], F32))
        ot_acc = ctx.enter_context(nc.psum_tensor("ot_acc", [P, KC, BANK], F32))

        y_loaded = sem("y_loaded")
        x_loaded = sem("x_loaded")
        wout_loaded = sem("wout_loaded")
        wout_ready = sem("wout_ready")
        w_loaded = [sem(f"w_loaded{s}") for s in range(RAW)]
        w_ready = sem("w_ready")
        adj_loaded = [sem(f"adj_loaded{s}") for s in range(ADJ)]
        mask_ready = sem("mask_ready")
        mask_counted = sem("mask_counted")
        bias_ready = sem("bias_ready")
        bias_used = sem("bias_used")
        ident_ready = sem("ident_ready")
        bank_full = sem("bank_full")
        bank_free = sem("bank_free")
        hi_ready = sem("hi_ready")
        shift_ready = sem("shift_ready")
        exp_ready = sem("exp_ready")
        masked_arg_ready = sem("masked_arg_ready")
        masked_exp_ready = sem("masked_exp_ready")
        ot_full = sem("ot_full")
        ot_hi_ready = sem("ot_hi_ready")
        ot_ready = sem("ot_ready")
        step = sem("step")
        pool_step = sem("pool_step")
        dve_gate = sem("dve_gate")
        pool_gate = sem("pool_gate")
        var_ready = sem("var_ready")
        std_ready = sem("std_ready")
        out_ready = sem("out_ready")
        stored = sem("stored")

        def bank_of(u):
            return ring[:, (u + X_USES) % RING, :]

        def two(ap):
            return ap.rearrange("p (a b) -> p a b", a=2)

        def split_of(u):
            if u < 0 or X_AT <= u < OUT_LAST_AT:
                kc = u + X_USES if u < 0 else u - X_AT
                return [xt[:, part, kc, :] for part in range(2)], bank_of(u)[:, 0:ROWS], 1.0
            if u in UNIT_USE:
                kind, c = UNITS[UNIT_USE.index(u)]
                if kind == "k":
                    dst = [kt[:, part, :, c * ROWS:(c + 1) * ROWS] for part in range(2)]
                elif kind == "v":
                    dst = [vv[:, part, 2 * c:2 * c + 2, :] for part in range(2)]
                else:
                    dst = [qt[:, part, :, c % 2 * ROWS:(c % 2 + 1) * ROWS] for part in range(2)]
                return dst, two(bank_of(u)), Q_SCALE if kind == "q" else 1.0
            j, = (u - at for at in PROBS_AT if at <= u < at + TILES)
            return [pt[:, j % PT, part, :] for part in range(2)], bank_of(u), 1.0

        def filled(h, u):
            return h * USES + (X_USES + u + 1)

        def freed(h, u):
            return h * USES + (X_USES + u + 1 + RING)

        def hi_number(h, u):
            return h * SPLITS + (X_USES + SPLIT_USES.index(u) + 1)

        block = ctx.enter_context(nc.Block())

        @block.sync
        def _(sp):
            def load_x(first_row):
                sp.dma_start(x_raw[:, :, :], x[bass.ds(first_row, ROWS), :].rearrange(
                    "(s p) d -> p s d", p=P)).then_inc(x_loaded, 16)

            load_x(0)
            for c in range(BLOCKS):
                sp.dma_start(y[:, 2 * c:2 * c + 2, :], x_rows[c]).then_inc(y_loaded, 16)
            with sp.Fori(0, HEADS) as h:
                sp.wait_ge(bank_full, filled(h, -1))
                load_x(((h + 1) % HEADS) * ROWS)
                for what, k in FEED:
                    if what == "adj":
                        t, s = k // 2, k % 2
                        sp.wait_ge(bias_ready, h * HALVES + k + 1)
                        sp.dma_start(adj_raw[:, k % ADJ, :], adj_rows[t // 2, t % 2, :, s * HALF:(s + 1) * HALF]
                                     ).then_inc(adj_loaded[k % ADJ], 16)
                    elif what == "w":
                        kind, c = UNITS[k]
                        sp.wait_ge(w_ready, h * NU + k + 1)
                        sp.dma_start(w_raw[:, k % RAW, :, :], weights[kind].rearrange(
                            "(k p) n -> p k n", p=P)[:, :, c * HIDDEN:(c + 1) * HIDDEN]
                                     ).then_inc(w_loaded[k % RAW], 16)
                    else:
                        sp.wait_ge(wout_ready, h + 1)
                        sp.dma_start(wout_raw[:, :, :], wout[bass.ds(h * HIDDEN, HIDDEN), :].rearrange(
                            "(k p) n -> p k n", p=P)).then_inc(wout_loaded, 16)
            for c in range(BLOCKS):
                sp.wait_ge(out_ready, c + 1)
                sp.dma_start(out_rows[c], y[:, 2 * c:2 * c + 2, :]).then_inc(stored, 16)
            sp.wait_ge(stored, 16 * BLOCKS)

        @block.gpsimd
        def _(pool):
            nc.gpsimd.memset(ident[:, :], 0.0).then_inc(pool_step, 1)
            pool.wait_ge(pool_step, 1)
            nc.gpsimd.affine_select(out=ident[:, :], in_=ident[:, :], compare_op=ALU.not_equal, fill=1.0, base=0,
                                    pattern=[[-1, P]], channel_multiplier=1).then_inc(ident_ready, 1)
            pool.sem_inc(bias_ready, ADJ)
            pool.sem_inc(w_ready, RAW)
            pool.sem_inc(wout_ready, 1)
            with pool.Fori(0, HEADS) as h:
                made = 0
                for what, k in FEED:
                    if what == "adj":
                        t, s = k // 2, k % 2
                        pool.wait_ge(mask_counted, h * HALVES + k + 1)
                        pool.wait_ge(bias_used, h * TILES + t + 1)
                        dst = bias[:, t % BIAS, :].rearrange("p (c i) -> p c i", c=BLOCKS)
                        nc.gpsimd.tensor_tensor(
                            dst[:, :, s * HJ:(s + 1) * HJ],
                            adj_raw[:, k % ADJ, :].rearrange("p (i c) -> p c i", c=BLOCKS),
                            mask[:, k % MASKS, :].rearrange("p (i c) -> p c i", c=BLOCKS),
                            ALU.add).then_inc(bias_ready, 1)
                        continue
                    made += 1
                    if what == "w":
                        src, dst, done = w_raw[:, k % RAW, :, :], w_split[:, k % SPLIT], w_ready
                        pool.wait_ge(w_loaded[k % RAW], h * (NU // RAW * 16) + (k // RAW + 1) * 16)
                        if k >= SPLIT:
                            pool.wait_ge(bank_full, filled(h, UNIT_USE[k - SPLIT]))
                    else:
                        src, dst, done = wout_raw[:, :, :], wout_split, wout_ready
                        pool.wait_ge(wout_loaded, h * 16 + 16)
                    pool.sem_inc(pool_gate, 1)
                    nc.gpsimd.tensor_copy(dst[:, 0, :, :], src).then_inc(pool_step, 1)
                    pool.wait_ge(pool_step, h * (NU + 1) + made + 1)
                    nc.gpsimd.tensor_tensor(dst[:, 1, :, :], src, dst[:, 0, :, :].bitcast(F32),
                                            ALU.subtract).then_inc(done, 1)

        @block.scalar
        def _(act):
            def hi_part(u):
                dst, src, factor = split_of(u)
                nc.scalar.activation(dst[0], src, ACT.Copy, scale=factor).then_inc(hi_ready, 1)

            for u in range(-X_USES, 0):
                act.wait_ge(bank_full, u + X_USES + 1)
                hi_part(u)
            with act.Fori(0, HEADS) as h:
                def split(first, end):
                    for u in range(first, end):
                        act.wait_ge(bank_full, filled(h, u))
                        hi_part(u)

                def count(t):
                    for k in (2 * t, 2 * t + 1):
                        act.wait_ge(mask_ready, h * HALVES + k + 1)
                        nc.scalar.activation(mask[:, k % MASKS, :], mask[:, k % MASKS, :], ACT.Copy,
                                             accum_out=masked_sum[:, t, k % 2:k % 2 + 1]).then_inc(mask_counted, 1)

                for t in range(BIAS):
                    count(t)
                split(K_AT, G_AT)
                for g in range(GROUPS):
                    for i in range(GROUP):
                        t = GROUP * g + i
                        if t + BIAS < TILES:
                            count(t + BIAS)
                        act.wait_ge(shift_ready, h * TILES + t + 1)
                        nc.scalar.activation(probs[:, i, :], probs[:, i, :], ACT.Exp, bias=shift[:, i:i + 1],
                                             scale=2.0, accum_out=exp_sum[:, i:i + 1]).then_inc(exp_ready, 1)
                    act.wait_ge(masked_arg_ready, h * GROUPS + g + 1)
                    nc.scalar.activation(masked_exp[:, :], masked_arg[:, :], ACT.Exp).then_inc(masked_exp_ready, 1)
                    split(Q_AT[g], OUT_AT[g])
                    split(PROBS_AT[g], PROBS_AT[g] + TILES)
                    for dc in range(KC):
                        act.wait_ge(ot_full, h * (GROUPS * KC) + g * KC + dc + 1)
                        nc.scalar.activation(ot[:, 0, dc, :], ot_acc[:, dc, :], ACT.Copy).then_inc(ot_hi_ready, 1)
                split(X_AT, OUT_LAST_AT)
            act.wait_ge(var_ready, 1)
            nc.scalar.activation(std[:, :], var_eps[:, :], ACT.Sqrt).then_inc(std_ready, 1)

        @block.tensor
        def _(pe):
            def turn_x(u):
                kc = u + X_USES if u < 0 else u - X_AT
                for s in range(ROWS // P):
                    last = nc.tensor.transpose(bank_of(u)[:, s * P:(s + 1) * P], x_raw[:, s, kc * P:(kc + 1) * P],
                                               ident[:, :])
                last.then_inc(bank_full, 1)

            def product(dst, lhs, rhs, first, last):
                nc.tensor.matmul(dst, lhs(1), rhs(0), start=first, stop=False)
                nc.tensor.matmul(dst, lhs(0), rhs(1), start=False, stop=False)
                return nc.tensor.matmul(dst, lhs(0), rhs(0), start=False, stop=last)

            pe.wait_ge(ident_ready, 1)
            pe.wait_ge(x_loaded, 16)
            for u in range(-X_USES, 0):
                turn_x(u)
            with pe.Fori(0, HEADS) as h:
                def free(u):
                    pe.wait_ge(bank_free, freed(h, u - RING))

                def project(k):
                    u = UNIT_USE[k]
                    free(u)
                    pe.wait_ge(w_ready, h * NU + k + 1 + RAW)
                    w, bank = w_split[:, k % SPLIT], two(bank_of(u))
                    for b in range(2):
                        cut = slice(b * P, (b + 1) * P)
                        for kc in range(KC):
                            def of_x(part, cols=slice(0, ROWS)):
                                return xt[:, part, kc, cols]

                            def of_w(part, cols=slice(0, HIDDEN)):
                                return w[:, part, kc, cols]

                            if UNITS[k][0] == "v":
                                last = product(bank[:, b, :], lambda n: of_x(n, cut), of_w, kc == 0, kc == KC - 1)
                            else:
                                last = product(bank[:, b, :], lambda n: of_w(n, cut), of_x, kc == 0, kc == KC - 1)
                    last.then_inc(bank_full, 1)

                def score(g):
                    for i in range(GROUP):
                        for m in range(CHUNKS):
                            u = SCORES_AT[g] + i * CHUNKS + m
                            free(u)
                            for dc in range(KC):
                                last = product(bank_of(u), lambda n: qt[:, n, dc, i * P:(i + 1) * P],
                                               lambda n: kt[:, n, dc, m * BANK:(m + 1) * BANK],
                                               dc == 0, dc == KC - 1)
                            last.then_inc(bank_full, 1)

                def out_product(g, u):
                    pe.wait_ge(ot_ready, h * (GROUPS * KC) + (g + 1) * KC)
                    for b in range(2):
                        free(u + b)
                        for n in range(2):
                            cut = slice((2 * b + n) * P, (2 * b + n + 1) * P)
                            for dc in range(KC):
                                last = product(two(bank_of(u + b))[:, n, :], lambda part: ot[:, part, dc, cut],
                                               lambda part: wout_split[:, part, dc, :], dc == 0, dc == KC - 1)
                        last.then_inc(bank_full, 1)

                def turn_probs(g, j):
                    free(PROBS_AT[g] + j)
                    for i in range(GROUP):
                        if j == 0:
                            pe.wait_ge(exp_ready, h * TILES + GROUP * g + i + 1)
                        last = nc.tensor.transpose(bank_of(PROBS_AT[g] + j)[:, i * P:(i + 1) * P],
                                                   probs[:, i, j * P:(j + 1) * P], ident[:, :])
                    last.then_inc(bank_full, 1)

                def weigh(g):
                    for j in range(PT - 1):
                        turn_probs(g, j)
                    for j in range(TILES):
                        if j + PT - 1 < TILES:
                            turn_probs(g, j + PT - 1)
                        pe.wait_ge(bank_free, freed(h, PROBS_AT[g] + j))
                        for dc in range(KC):
                            last = product(ot_acc[:, dc, :], lambda n: vv[:, n, j, dc * P:(dc + 1) * P],
                                           lambda n: pt[:, j % PT, n, :], j == 0, j == TILES - 1)
                            if j == TILES - 1:
                                last.then_inc(ot_full, 1)

                pe.wait_ge(bank_free, freed(h, -1))
                for k in range(G_AT):
                    project(k)
                for g in range(GROUPS):
                    pe.wait_ge(bank_free, freed(h, V_AT - 1 if g == 0 else Q_AT[g - 1] + 1))
                    score(g)
                    if g < GROUPS - 1:
                        project(G_AT + 2 * g)
                        project(G_AT + 2 * g + 1)
                    if g:
                        if g == 1:
                            pe.wait_ge(wout_ready, h + 2)
                        out_product(g - 1, OUT_AT[g])
                    weigh(g)
                pe.wait_ge(x_loaded, h * 16 + 32)
                for u in range(X_AT, OUT_LAST_AT):
                    free(u)
                    turn_x(u)
                out_product(GROUPS - 1, OUT_LAST_AT)

        @block.vector
        def _(dve):
            def lo_part(u):
                dst, src, factor = split_of(u)
                nc.vector.scalar_tensor_tensor(out=dst[1], in0=src, scalar=factor, in1=dst[0].bitcast(F32),
                                               op0=ALU.mult, op1=ALU.subtract).then_inc(bank_free, 1)

            dve.sem_inc(bank_free, RING)
            dve.sem_inc(bias_used, BIAS)
            for u in range(-X_USES, 0):
                dve.wait_ge(hi_ready, u + X_USES + 1)
                lo_part(u)
            dve.wait_ge(y_loaded, 16 * BLOCKS)
            TILE_STEPS, GROUP_STEPS = 2, 4
            STEPS = GROUPS * (GROUP * TILE_STEPS + GROUP_STEPS)
            with dve.Fori(0, HEADS) as h:
                def split(first, end):
                    for u in range(first, end):
                        dve.wait_ge(hi_ready, hi_number(h, u))
                        lo_part(u)

                def write_masks(t):
                    for k in (2 * t, 2 * t + 1):
                        dve.wait_ge(adj_loaded[k % ADJ], h * (HALVES // ADJ * 16) + (k // ADJ + 1) * 16)
                        dve.wait_ge(bias_ready, h * HALVES + (k - MASKS + 1 + ADJ))
                        nc.vector.tensor_scalar(mask[:, k % MASKS, :], adj_raw[:, k % ADJ, :], 0.0, BIG,
                                                ALU.is_equal, ALU.mult).then_inc(mask_ready, 1)

                def bias_scores(g, i):
                    t = GROUP * g + i
                    steps = g * (GROUP * TILE_STEPS + GROUP_STEPS) + i * TILE_STEPS
                    dve.wait_ge(mask_counted, h * HALVES + 2 * t + 2)
                    nc.vector.tensor_scalar(unmasked[:, :], masked_sum[:, t, 0:1], masked_sum[:, t, 1:2], 0.0,
                                            ALU.add, ALU.is_equal).then_inc(step, 1)
                    for m in range(CHUNKS):
                        u = SCORES_AT[g] + i * CHUNKS + m
                        if m == 0:
                            dve.wait_ge(bias_ready, h * HALVES + (2 * t + 2 + ADJ))
                        dve.wait_ge(bank_full, filled(h, u))
                        dve.sem_inc(dve_gate, 1)
                        nc.vector.tensor_tensor_reduce(
                            probs[:, i, m * BANK:(m + 1) * BANK], bank_of(u),
                            bias[:, t % BIAS, m * BANK:(m + 1) * BANK], 1.0, -3.0e38, ALU.add, ALU.max,
                            maxima[:, m:m + 1]).then_inc(bank_free, 1)
                        if m == 1:
                            dve.wait_ge(step, h * STEPS + steps + 1)
                            nc.vector.tensor_scalar(maxima[:, CHUNKS:CHUNKS + 1], unmasked[:, :], NONE, MASKED / 2,
                                                    ALU.mult, ALU.min).then_inc(step, 1)
                    dve.wait_ge(step, h * STEPS + steps + 2)
                    dve.wait_ge(bank_free, freed(h, SCORES_AT[g] + (i + 1) * CHUNKS - 1))
                    nc.vector.tensor_reduce(top[:, :], maxima[:, :], AX.X, ALU.max).then_inc(bias_used, 1)
                    dve.wait_ge(bias_used, h * TILES + (t + 1 + BIAS))
                    nc.vector.tensor_scalar(shift[:, i:i + 1], top[:, :], -2.0, None, ALU.mult
                                            ).then_inc(shift_ready, 1)

                def invert_denominators(g):
                    steps = g * (GROUP * TILE_STEPS + GROUP_STEPS) + GROUP * TILE_STEPS
                    nc.vector.tensor_tensor(total_masked[:, :], masked_sum[:, GROUP * g:GROUP * (g + 1), 0],
                                            masked_sum[:, GROUP * g:GROUP * (g + 1), 1], ALU.add).then_inc(step, 1)
                    dve.wait_ge(step, h * STEPS + steps + 1)
                    dve.wait_ge(masked_exp_ready, h * GROUPS + g + 1)
                    nc.vector.scalar_tensor_tensor(out=masked_part[:, :], in0=total_masked[:, :], scalar=1.0 / BIG,
                                                   in1=masked_exp[:, :], op0=ALU.mult, op1=ALU.mult
                                                   ).then_inc(step, 1)
                    dve.wait_ge(step, h * STEPS + steps + 2)
                    dve.wait_ge(exp_ready, h * TILES + GROUP * (g + 1))
                    nc.vector.tensor_tensor(denom[:, :], masked_part[:, :], exp_sum[:, :], ALU.add
                                            ).then_inc(step, 1)
                    dve.wait_ge(step, h * STEPS + steps + 3)
                    nc.vector.reciprocal(inv_denom[:, :], denom[:, :]).then_inc(step, 1)

                def add_output(g, u):
                    dve.wait_ge(step, h * STEPS + (g + 1) * (GROUP * TILE_STEPS + GROUP_STEPS))
                    for b in range(2):
                        dve.wait_ge(bank_full, filled(h, u + b))
                        for n in range(2):
                            i = 2 * b + n
                            rows = y[:, GROUP * g + i, :]
                            last = nc.vector.scalar_tensor_tensor(
                                out=rows, in0=two(bank_of(u + b))[:, n, :], scalar=inv_denom[:, i:i + 1], in1=rows,
                                op0=ALU.mult, op1=ALU.add)
                        last.then_inc(bank_free, 1)

                for t in range(BIAS):
                    write_masks(t)
                split(K_AT, G_AT)
                for g in range(GROUPS):
                    for i in range(GROUP):
                        bias_scores(g, i)
                        if GROUP * g + i + BIAS < TILES:
                            write_masks(GROUP * g + i + BIAS)
                    dve.wait_ge(shift_ready, h * TILES + GROUP * (g + 1))
                    nc.vector.tensor_scalar(masked_arg[:, :], shift[:, :], MASKED, 0.0, ALU.add, ALU.min
                                            ).then_inc(masked_arg_ready, 1)
                    split(Q_AT[g], OUT_AT[g])
                    if g:
                        add_output(g - 1, OUT_AT[g])
                    split(PROBS_AT[g], PROBS_AT[g] + TILES)
                    invert_denominators(g)
                    for dc in range(KC):
                        dve.wait_ge(ot_hi_ready, h * (GROUPS * KC) + g * KC + dc + 1)
                        nc.vector.scalar_tensor_tensor(out=ot[:, 1, dc, :], in0=ot_acc[:, dc, :], scalar=1.0,
                                                       in1=ot[:, 0, dc, :].bitcast(F32), op0=ALU.mult,
                                                       op1=ALU.subtract).then_inc(ot_ready, 1)
                split(X_AT, OUT_LAST_AT)
                add_output(GROUPS - 1, OUT_LAST_AT)

            done = HEADS * STEPS
            dve.wait_ge(bank_free, HEADS * USES + X_USES + RING)
            for t in range(TILES):
                nc.vector.bn_stats(stats[:, t, :], y[:, t, :]).then_inc(step, 1)
            for t in range(TILES):
                dve.wait_ge(step, done + t + 1)
                nc.vector.bn_aggr(moments[:, t, :], stats[:, t, :]).then_inc(step, 1)
            dve.wait_ge(step, done + 2 * TILES)
            nc.vector.tensor_scalar(var_eps[:, :], moments[:, :, 1], EPS, None, ALU.add).then_inc(var_ready, 1)
            dve.wait_ge(std_ready, 1)
            nc.vector.reciprocal(inv_std[:, :], std[:, :]).then_inc(step, 1)
            dve.wait_ge(step, done + 2 * TILES + 1)
            for t in range(TILES):
                last = nc.vector.tensor_scalar(y[:, t, :], y[:, t, :], moments[:, t, 0:1], inv_std[:, t:t + 1],
                                               ALU.subtract, ALU.mult)
                if t % 2:
                    last.then_inc(out_ready, 1)


def kernel(x, adj, L0_gnn_Wq, L0_gnn_Wk, L0_gnn_Wv, L0_gnn_Wout):
    import concourse.bacc as bacc
    from concourse.bass_utils import run_bass_kernel_spmd

    nc = bacc.Bacc("TRN2", target_bir_lowering=False, num_devices=1)
    arrays = {"x": x, "adj": adj, "wq": L0_gnn_Wq, "wk": L0_gnn_Wk, "wv": L0_gnn_Wv, "wout": L0_gnn_Wout}
    arrays = {name: np.ascontiguousarray(a) for name, a in arrays.items()}
    aps = [nc.dram_tensor(name, a.shape, mybir.dt.from_np(a.dtype), kind="ExternalInput").ap()
           for name, a in arrays.items()]
    out = nc.dram_tensor("out", (N, HIDDEN), F32, kind="ExternalOutput").ap()
    build(nc, *aps, out)
    return run_bass_kernel_spmd(nc, [arrays], core_ids=[0]).results[0]["out"]
```

```python
from contextlib import ExitStack

import numpy as np
import concourse.bass as bass
from concourse import mybir

ALU = mybir.AluOpType
ACT = mybir.ActivationFunctionType
AX = mybir.AxisListType
F32 = mybir.dt.float32
F32R = mybir.dt.float32r

P = 128
HIDDEN = 256
HEADS = 8
N = 2048
ROWS = N // HEADS
BLOCKS = N // ROWS
KC = HIDDEN // P
TILES = N // P
GROUP = 4
GROUPS = TILES // GROUP
GN = GROUP * P
BANK = 512
CHUNKS = N // BANK
HALF = N // 2
HJ = HALF // BLOCKS

EPS = 1e-5
MASKED = -1.0e6
BIG = -(2.0 ** 100)
NONE = -1.0e38
Q_SCALE = HIDDEN ** -0.5 / 2

UNITS = ([("v", c) for c in range(6)] + [("q", 2), ("q", 3)] + [("v", c) for c in range(6, BLOCKS)]
         + [("q", c) for c in range(4, BLOCKS)] + [("k", c) for c in range(BLOCKS)] + [("q", 0), ("q", 1)])
NU = len(UNITS)
AHEAD = list(range(NU - BLOCKS - 2, NU))

RING = 6
RAW = 3
SPLIT = 2
BIAS = 4
PT = 3
MASKS = 2


def schedule():
    units = iter(range(NU))

    def unit():
        return ("unit", next(units))

    steps = []
    for g in range(GROUPS):
        for i in range(GROUP):
            for m in range(CHUNKS):
                steps.append(("score", g, i, m))
                if g == 0 and m % 2 and (i, m) < (GROUP - 1, 0):
                    steps.append(unit())
        steps += [("wout",)] if g == 0 else []
        steps += [unit(), unit()]
        steps += [("out", g - 1, 0) if g else unit(), ("turn", g, 0)]
        steps += [("out", g - 1, 1) if g else unit(), ("turn", g, 1)]
        for j in range(TILES):
            steps += [("turn", g, j + PT - 1)] if j + PT - 1 < TILES else []
            steps.append(("weigh", g, j))
            if g == GROUPS - 1 and j % 2 and j < 12:
                steps.append(unit())
        if g == GROUPS - 2:
            steps += [("x", kc) for kc in range(KC)]
    return steps + [("unit", k) for k in units] + [("out", GROUPS - 1, b) for b in range(2)]


HEAD = schedule()
START = [("x", kc) for kc in range(KC)] + [("unit", k) for k in AHEAD]
HANDED = ("score", "unit", "x", "out", "turn")
HALVED = ("unit", "x", "turn")


def numbers(steps, kinds):
    return {s: n for n, s in enumerate([s for s in steps if s[0] in kinds])}


BANK_NO, START_BANK_NO = numbers(HEAD, HANDED), numbers(START, HANDED)
HI_NO, START_HI_NO = numbers(HEAD, HALVED), numbers(START, HALVED)
BANKS, START_BANKS = len(BANK_NO), len(START_BANK_NO)
HIS, START_HIS = len(HI_NO), len(START_HI_NO)
START_UNITS = len(AHEAD)
assert BANKS % RING == 0 and START_BANKS % RING == 0 and NU % RAW == 0 and NU % SPLIT == 0


def build(nc, x, adj, wq, wk, wv, wout, out):
    adj_rows = adj.rearrange("(s p c) m -> c s p m", p=P, c=BLOCKS)
    x_rows = x.rearrange("(s p c) d -> c p s d", p=P, c=BLOCKS)
    out_rows = out.rearrange("(s p c) d -> c p s d", p=P, c=BLOCKS)
    weights = {"q": wq, "k": wk, "v": wv}
    bias_kept = nc.dram_tensor("bias_kept", (TILES, P, N), F32, kind="Internal").ap()

    with ExitStack() as ctx:
        def sb(name, shape, dt=F32):
            return ctx.enter_context(nc.sbuf_tensor(name, shape, dt))

        def sem(name):
            return ctx.enter_context(nc.semaphore(name))

        kt = sb("kt", [P, 2, KC, N], F32R)
        vv = sb("vv", [P, 2, TILES, HIDDEN], F32R)
        qt = sb("qt", [P, 2, KC, GN], F32R)
        xt = sb("xt", [P, 2, KC, ROWS], F32R)
        pt = sb("pt", [P, PT, 2, GN], F32R)
        ot = sb("ot", [P, 2, KC, GN], F32R)
        w_split = sb("w_split", [P, SPLIT, 2, KC, HIDDEN], F32R)
        wout_split = sb("wout_split", [P, 2, KC, HIDDEN], F32R)
        w_raw = sb("w_raw", [P, RAW, KC, HIDDEN])
        wout_raw = sb("wout_raw", [P, KC, HIDDEN])
        x_raw = sb("x_raw", [P, ROWS // P, HIDDEN])
        bias = sb("bias", [P, BIAS, N])
        mask = sb("mask", [P, MASKS, HALF])
        probs = sb("probs", [P, GROUP, N])
        y = sb("y", [P, TILES, HIDDEN])
        ident = sb("ident", [P, P])
        maxima = sb("maxima", [P, CHUNKS])
        top = sb("top", [P, 1])
        shift = sb("shift", [P, GROUP])
        masked_sum = sb("masked_sum", [P, TILES, 2])
        unmasked = sb("unmasked", [P, 1])
        floor = sb("floor", [P, TILES])
        masked = sb("masked", [P, TILES])
        exp_sum = sb("exp_sum", [P, GROUP])
        masked_arg = sb("masked_arg", [P, GROUP])
        masked_exp = sb("masked_exp", [P, GROUP])
        masked_part = sb("masked_part", [P, GROUP])
        denom = sb("denom", [P, GROUP])
        inv_denom = sb("inv_denom", [P, GROUP])
        stats = sb("stats", [P, TILES, 6])
        moments = sb("moments", [P, TILES, 2])
        var_eps = sb("var_eps", [P, TILES])
        std = sb("std", [P, TILES])
        inv_std = sb("inv_std", [P, TILES])

        ring = ctx.enter_context(nc.psum_tensor("ring", [P, RING, BANK], F32))
        ot_acc = ctx.enter_context(nc.psum_tensor("ot_acc", [P, KC, BANK], F32))

        y_loaded = sem("y_loaded")
        x_loaded = sem("x_loaded")
        wout_loaded = sem("wout_loaded")
        wout_hi_ready = sem("wout_hi_ready")
        wout_ready = sem("wout_ready")
        w_loaded = [sem(f"w_loaded{s}") for s in range(RAW)]
        w_hi_ready = sem("w_hi_ready")
        w_ready = sem("w_ready")
        adj_loaded = [sem(f"adj_loaded{s}") for s in range(4)]
        mask_ready = sem("mask_ready")
        mask_counted = sem("mask_counted")
        bias_ready = {"pool": sem("bias_ready_pool"), "dve": sem("bias_ready_dve")}
        bias_stored = [sem(f"bias_stored{s}") for s in range(2)]
        bias_loaded = [sem(f"bias_loaded{s}") for s in range(BIAS)]
        bias_used = sem("bias_used")
        ident_ready = sem("ident_ready")
        bank_full = sem("bank_full")
        bank_free = sem("bank_free")
        hi_ready = sem("hi_ready")
        shift_ready = sem("shift_ready")
        exp_ready = sem("exp_ready")
        masked_arg_ready = sem("masked_arg_ready")
        masked_exp_ready = sem("masked_exp_ready")
        ot_full = sem("ot_full")
        ot_hi_ready = sem("ot_hi_ready")
        ot_ready = sem("ot_ready")
        step = sem("step")
        first_step = sem("first_step")
        pool_step = sem("pool_step")
        dve_gate = sem("dve_gate")
        var_ready = sem("var_ready")
        std_ready = sem("std_ready")
        out_ready = sem("out_ready")
        stored = sem("stored")

        def bank_no(h, s):
            return START_BANK_NO[s] + 1 if h is None else h * BANKS + (START_BANKS + BANK_NO[s] + 1)

        def hi_no(h, s):
            return START_HI_NO[s] + 1 if h is None else h * HIS + (START_HIS + HI_NO[s] + 1)

        def unit_no(h, k):
            return AHEAD.index(k) + 1 if h is None else h * NU + (START_UNITS + k + 1)

        def unit_slot(h, k, slots):
            return (AHEAD.index(k) if h is None else START_UNITS + k) % slots

        def unit_loads(h, k):
            n = AHEAD.index(k) if h is None else START_UNITS + k
            return (n // RAW + 1) * 16 if h is None else h * (NU // RAW * 16) + (n // RAW + 1) * 16

        def bank_of(h, s):
            return ring[:, (START_BANK_NO if h is None else BANK_NO)[s] % RING, :]

        def two(ap):
            return ap.rearrange("p (a b) -> p a b", a=2)

        def split_of(h, s):
            if s[0] == "x":
                return [xt[:, part, s[1], :] for part in range(2)], bank_of(h, s)[:, 0:ROWS], 1.0
            if s[0] == "turn":
                return [pt[:, s[2] % PT, part, :] for part in range(2)], bank_of(h, s), 1.0
            kind, c = UNITS[s[1]]
            if kind == "k":
                dst = [kt[:, part, :, c * ROWS:(c + 1) * ROWS] for part in range(2)]
            elif kind == "v":
                dst = [vv[:, part, 2 * c:2 * c + 2, :] for part in range(2)]
            else:
                dst = [qt[:, part, :, c % 2 * ROWS:(c % 2 + 1) * ROWS] for part in range(2)]
            return dst, two(bank_of(h, s)), Q_SCALE if kind == "q" else 1.0

        def tile_ends(s):
            return s[0] == "score" and s[3] == CHUNKS - 1

        def bias_slot(first, t):
            return bias[:, t % 2 if first else t % BIAS, :]

        def adj_slot(k):
            return bias[:, 2 + k % 4 // 2, k % 2 * HALF:(k % 2 + 1) * HALF]

        def maker(k):
            return "dve" if k % 2 or k < 4 else "pool"

        def wait_for_bias(eng, k):
            eng.wait_ge(bias_ready[maker(k)], sum(maker(n) == maker(k) for n in range(k + 1)))

        def add_bias(eng, k):
            t = k // 2
            eng.wait_ge(mask_counted, k + 1)
            if t >= 2:
                eng.wait_ge(bias_used, BIAS + t - 1)
                eng.wait_ge(bias_stored[t % 2], 16 * (t // 2))
            dst = bias_slot(True, t).rearrange("p (c i) -> p c i", c=BLOCKS)
            eng.tensor_tensor(dst[:, :, k % 2 * HJ:(k % 2 + 1) * HJ],
                              adj_slot(k).rearrange("p (i c) -> p c i", c=BLOCKS),
                              mask[:, k % MASKS, :].rearrange("p (i c) -> p c i", c=BLOCKS),
                              ALU.add).then_inc(bias_ready[maker(k)], 1)

        block = ctx.enter_context(nc.Block())

        @block.sync
        def _(sp):
            def load_x(first_row):
                sp.dma_start(x_raw[:, :, :], x[bass.ds(first_row, ROWS), :].rearrange(
                    "(s p) d -> p s d", p=P)).then_inc(x_loaded, 16)

            def load_unit(h, k):
                kind, c = UNITS[k]
                sp.wait_ge(w_ready, unit_no(h, k))
                sp.dma_start(w_raw[:, unit_slot(h, k, RAW), :, :], weights[kind].rearrange(
                    "(k p) n -> p k n", p=P)[:, :, c * HIDDEN:(c + 1) * HIDDEN]
                             ).then_inc(w_loaded[unit_slot(h, k, RAW)], 16)

            def load_adj(k):
                if k >= 4:
                    wait_for_bias(sp, k - 4)
                sp.dma_start(adj_slot(k), adj_rows[k // 4, k // 2 % 2, :, k % 2 * HALF:(k % 2 + 1) * HALF]
                             ).then_inc(adj_loaded[k % 4], 16)

            def store_bias(t):
                for k in (2 * t, 2 * t + 1):
                    wait_for_bias(sp, k)
                sp.dma_start(bias_kept[t], bias_slot(True, t)).then_inc(bias_stored[t % 2], 16)

            def load_bias(h, t):
                sp.wait_ge(bias_used, h * TILES + t + 1)
                sp.dma_start(bias_slot(False, t), bias_kept[t]).then_inc(bias_loaded[t % BIAS], 16)

            def begin(h):
                sp.wait_ge(bank_full, h * BANKS + START_BANKS)
                load_x(((h + 1) % HEADS) * ROWS)
                sp.wait_ge(wout_ready, h + 1)
                sp.dma_start(wout_raw[:, :, :], wout[bass.ds(h * HIDDEN, HIDDEN), :].rearrange(
                    "(k p) n -> p k n", p=P)).then_inc(wout_loaded, 16)

            def feed(h, s, first=False):
                if s[0] == "unit" and s[1] + RAW + SPLIT < NU:
                    load_unit(h, s[1] + RAW + SPLIT)
                if tile_ends(s):
                    t = GROUP * s[1] + s[2]
                    if first:
                        store_bias(t)
                        if t + 2 < TILES:
                            load_adj(2 * t + 4)
                            load_adj(2 * t + 5)
                    elif t + BIAS < TILES:
                        load_bias(h, t + BIAS)

            last_scores = HEAD.index(("score", GROUPS - 1, GROUP - 1, CHUNKS - 1))
            before, behind = HEAD[:last_scores + 1], HEAD[last_scores + 1:]

            load_x(0)
            for n, k in enumerate(AHEAD):
                load_unit(None, k)
                if n in (1, 2, 3, 4):
                    load_adj(n - 1)
            for c in range(BLOCKS):
                sp.dma_start(y[:, 2 * c:2 * c + 2, :], x_rows[c]).then_inc(y_loaded, 16)
            for k in range(RAW + SPLIT):
                load_unit(0, k)
            begin(0)
            for s in before:
                feed(0, s, True)
            for s in range(2):
                sp.wait_ge(bias_stored[s], 16 * (TILES // 2))
            sp.wait_ge(bias_used, BIAS + TILES)
            with sp.Fori(1, HEADS) as h:
                coming = iter(range(BIAS))
                for s in behind:
                    feed(h - 1, s)
                    if s[0] == "turn" and s[2] < BIAS:
                        load_bias(h, next(coming))
                for k in range(RAW + SPLIT):
                    load_unit(h, k)
                begin(h)
                for s in before:
                    feed(h, s)
            for s in behind:
                feed(HEADS - 1, s)
            for c in range(BLOCKS):
                sp.wait_ge(out_ready, c + 1)
                sp.dma_start(out_rows[c], y[:, 2 * c:2 * c + 2, :]).then_inc(stored, 16)
            sp.wait_ge(stored, 16 * BLOCKS)

        @block.gpsimd
        def _(pool):
            def lo_unit(h, k):
                s, r = unit_slot(h, k, SPLIT), unit_slot(h, k, RAW)
                pool.wait_ge(w_hi_ready, unit_no(h, k))
                nc.gpsimd.tensor_tensor(w_split[:, s, 1, :, :], w_raw[:, r, :, :],
                                        w_split[:, s, 0, :, :].bitcast(F32), ALU.subtract).then_inc(w_ready, 1)

            def head(h, first):
                for k in range(SPLIT):
                    lo_unit(h, k)
                for s in HEAD:
                    if s[0] == "unit" and s[1] + SPLIT < NU:
                        lo_unit(h, s[1] + SPLIT)
                    elif s[0] == "wout":
                        pool.wait_ge(wout_hi_ready, h + 1)
                        nc.gpsimd.tensor_tensor(wout_split[:, 1, :, :], wout_raw[:, :, :],
                                                wout_split[:, 0, :, :].bitcast(F32), ALU.subtract
                                                ).then_inc(wout_ready, 1)
                    elif first and tile_ends(s) and GROUP * s[1] + s[2] + 2 < TILES:
                        add_bias(nc.gpsimd, 2 * (GROUP * s[1] + s[2]) + 4)

            nc.gpsimd.memset(ident[:, :], 0.0).then_inc(pool_step, 1)
            pool.wait_ge(pool_step, 1)
            nc.gpsimd.affine_select(out=ident[:, :], in_=ident[:, :], compare_op=ALU.not_equal, fill=1.0, base=0,
                                    pattern=[[-1, P]], channel_multiplier=1).then_inc(ident_ready, 1)
            pool.sem_inc(w_ready, RAW)
            pool.sem_inc(wout_ready, 1)
            for k in AHEAD:
                lo_unit(None, k)
            head(0, True)
            with pool.Fori(1, HEADS) as h:
                head(h, False)

        @block.scalar
        def _(act):
            def hi_unit(h, k):
                s, r = unit_slot(h, k, SPLIT), unit_slot(h, k, RAW)
                act.wait_ge(w_loaded[r], unit_loads(h, k))
                nc.scalar.activation(w_split[:, s, 0, :, :], w_raw[:, r, :, :], ACT.Copy).then_inc(w_hi_ready, 1)

            def hi_part(h, s):
                dst, src, factor = split_of(h, s)
                act.wait_ge(bank_full, bank_no(h, s))
                nc.scalar.activation(dst[0], src, ACT.Copy, scale=factor).then_inc(hi_ready, 1)

            def count(t):
                for k in (2 * t, 2 * t + 1):
                    act.wait_ge(mask_ready, k + 1)
                    nc.scalar.activation(mask[:, k % MASKS, :], mask[:, k % MASKS, :], ACT.Copy,
                                         accum_out=masked_sum[:, t, k % 2:k % 2 + 1]).then_inc(mask_counted, 1)

            def head(h, first):
                for k in range(SPLIT):
                    hi_unit(h, k)
                for s in HEAD:
                    if s[0] in HALVED:
                        hi_part(h, s)
                    if s[0] == "unit" and s[1] + SPLIT < NU:
                        hi_unit(h, s[1] + SPLIT)
                    elif s[0] == "wout":
                        act.wait_ge(wout_loaded, h * 16 + 16)
                        nc.scalar.activation(wout_split[:, 0, :, :], wout_raw[:, :, :], ACT.Copy
                                             ).then_inc(wout_hi_ready, 1)
                    elif tile_ends(s):
                        g, i = s[1], s[2]
                        t = GROUP * g + i
                        if first and t + 2 < TILES:
                            count(t + 2)
                        act.wait_ge(shift_ready, h * TILES + t + 1)
                        nc.scalar.activation(probs[:, i, :], probs[:, i, :], ACT.Exp, bias=shift[:, i:i + 1],
                                             scale=2.0, accum_out=exp_sum[:, i:i + 1]).then_inc(exp_ready, 1)
                        if i == GROUP - 1:
                            act.wait_ge(masked_arg_ready, h * GROUPS + g + 1)
                            nc.scalar.activation(masked_exp[:, :], masked_arg[:, :], ACT.Exp
                                                 ).then_inc(masked_exp_ready, 1)
                    elif s[0] == "weigh" and s[2] == TILES - 1:
                        for dc in range(KC):
                            act.wait_ge(ot_full, h * (GROUPS * KC) + s[1] * KC + dc + 1)
                            nc.scalar.activation(ot[:, 0, dc, :], ot_acc[:, dc, :], ACT.Copy
                                                 ).then_inc(ot_hi_ready, 1)

            for k in AHEAD[:SPLIT]:
                hi_unit(None, k)
            for n, s in enumerate(START):
                hi_part(None, s)
                if s[0] == "unit" and s[1] + SPLIT < NU:
                    hi_unit(None, s[1] + SPLIT)
                if n in (4, 7):
                    count(n // 3 - 1)
            head(0, True)
            with act.Fori(1, HEADS) as h:
                head(h, False)
            act.wait_ge(var_ready, 1)
            nc.scalar.activation(std[:, :], var_eps[:, :], ACT.Sqrt).then_inc(std_ready, 1)

        @block.tensor
        def _(pe):
            def product(dst, lhs, rhs, first, last):
                nc.tensor.matmul(dst, lhs(1), rhs(0), start=first, stop=False)
                nc.tensor.matmul(dst, lhs(0), rhs(1), start=False, stop=False)
                return nc.tensor.matmul(dst, lhs(0), rhs(0), start=False, stop=last)

            def turn_x(bank, kc):
                for n in range(ROWS // P):
                    last = nc.tensor.transpose(bank[:, n * P:(n + 1) * P], x_raw[:, n, kc * P:(kc + 1) * P],
                                               ident[:, :])
                return last

            def project(h, bank, k):
                pe.wait_ge(w_ready, unit_no(h, k) + RAW)
                w = w_split[:, unit_slot(h, k, SPLIT)]
                for b in range(2):
                    cut = slice(b * P, (b + 1) * P)
                    for kc in range(KC):
                        def of_x(part, cols=slice(0, ROWS)):
                            return xt[:, part, kc, cols]

                        def of_w(part, cols=slice(0, HIDDEN)):
                            return w[:, part, kc, cols]

                        if UNITS[k][0] == "v":
                            last = product(two(bank)[:, b, :], lambda n: of_x(n, cut), of_w, kc == 0, kc == KC - 1)
                        else:
                            last = product(two(bank)[:, b, :], lambda n: of_w(n, cut), of_x, kc == 0, kc == KC - 1)
                return last

            def score(h, first, bank, g, i, m):
                if i == m == 0:
                    if g:
                        pe.wait_ge(bank_free, bank_no(h, ("unit", UNITS.index(("q", 2 * g + 1)))) + RING)
                    else:
                        pe.wait_ge(bank_free, h * BANKS + (START_BANKS + RING - (0 if first else 2)))
                for dc in range(KC):
                    last = product(bank, lambda n: qt[:, n, dc, i * P:(i + 1) * P],
                                   lambda n: kt[:, n, dc, m * BANK:(m + 1) * BANK], dc == 0, dc == KC - 1)
                return last

            def out_product(h, bank, g, b):
                if b == 0:
                    pe.wait_ge(ot_ready, h * (GROUPS * KC) + (g + 1) * KC)
                    pe.wait_ge(wout_ready, h + 2)
                for n in range(2):
                    cut = slice((2 * b + n) * P, (2 * b + n + 1) * P)
                    for dc in range(KC):
                        last = product(two(bank)[:, n, :], lambda part: ot[:, part, dc, cut],
                                       lambda part: wout_split[:, part, dc, :], dc == 0, dc == KC - 1)
                return last

            def turn_probs(h, bank, g, j):
                for i in range(GROUP):
                    if j == 0:
                        pe.wait_ge(exp_ready, h * TILES + GROUP * g + i + 1)
                    last = nc.tensor.transpose(bank[:, i * P:(i + 1) * P], probs[:, i, j * P:(j + 1) * P],
                                               ident[:, :])
                return last

            def weigh(h, g, j):
                pe.wait_ge(bank_free, bank_no(h, ("turn", g, j)) + RING)
                for dc in range(KC):
                    last = product(ot_acc[:, dc, :], lambda n: vv[:, n, j, dc * P:(dc + 1) * P],
                                   lambda n: pt[:, j % PT, n, :], j == 0, j == TILES - 1)
                    if j == TILES - 1:
                        last.then_inc(ot_full, 1)

            def run(h, steps, first=True):
                for s in steps:
                    if s[0] in HANDED:
                        bank = bank_of(h, s)
                        pe.wait_ge(bank_free, bank_no(h, s))
                    if s[0] == "x":
                        if s[1] == 0:
                            pe.wait_ge(x_loaded, 16 if h is None else h * 16 + 32)
                        turn_x(bank, s[1]).then_inc(bank_full, 1)
                    elif s[0] == "unit":
                        if s[1] == AHEAD[0]:
                            pe.wait_ge(bank_free, bank_no(h, ("x", KC - 1)) + RING)
                        project(h, bank, s[1]).then_inc(bank_full, 1)
                    elif s[0] == "score":
                        score(h, first, bank, *s[1:]).then_inc(bank_full, 1)
                    elif s[0] == "out":
                        out_product(h, bank, *s[1:]).then_inc(bank_full, 1)
                    elif s[0] == "turn":
                        turn_probs(h, bank, *s[1:]).then_inc(bank_full, 1)
                    elif s[0] == "weigh":
                        weigh(h, *s[1:])

            pe.wait_ge(ident_ready, 1)
            run(None, START)
            run(0, HEAD)
            with pe.Fori(1, HEADS) as h:
                run(h, HEAD, False)

        @block.vector
        def _(dve):
            GROUP_STEPS = 3
            STEPS = GROUPS * GROUP_STEPS
            made = [0]

            def own(ins):
                made[0] += 1
                ins.then_inc(first_step, 1)
                dve.wait_ge(first_step, made[0])

            def lo_part(h, s):
                dst, src, factor = split_of(h, s)
                dve.wait_ge(hi_ready, hi_no(h, s))
                nc.vector.scalar_tensor_tensor(out=dst[1], in0=src, scalar=factor, in1=dst[0].bitcast(F32),
                                               op0=ALU.mult, op1=ALU.subtract).then_inc(bank_free, 1)

            def write_masks(t):
                for k in (2 * t, 2 * t + 1):
                    dve.wait_ge(adj_loaded[k % 4], (k // 4 + 1) * 16)
                    if k >= MASKS:
                        wait_for_bias(dve, k - MASKS)
                    nc.vector.tensor_scalar(mask[:, k % MASKS, :], adj_slot(k), 0.0, BIG, ALU.is_equal, ALU.mult
                                            ).then_inc(mask_ready, 1)

            def find_floor(t):
                dve.wait_ge(mask_counted, 2 * t + 2)
                own(nc.vector.tensor_scalar(unmasked[:, :], masked_sum[:, t, 0:1], masked_sum[:, t, 1:2], 0.0,
                                            ALU.add, ALU.is_equal))
                own(nc.vector.tensor_scalar(floor[:, t:t + 1], unmasked[:, :], NONE, MASKED / 2, ALU.mult, ALU.min))

            def bias_scores(h, first, s):
                g, i, m = s[1:]
                t = GROUP * g + i
                if m == 0:
                    if first:
                        find_floor(t)
                        for k in (2 * t, 2 * t + 1):
                            wait_for_bias(dve, k)
                    else:
                        dve.wait_ge(bias_loaded[t % BIAS], h * (TILES // BIAS * 16)
                                    + (t // BIAS + 1 - TILES // BIAS) * 16)
                dve.wait_ge(bank_full, bank_no(h, s))
                dve.sem_inc(dve_gate, 1)
                cut = slice(m * BANK, (m + 1) * BANK)
                nc.vector.tensor_tensor_reduce(probs[:, i, cut], bank_of(h, s), bias_slot(first, t)[:, cut],
                                               1.0, floor[:, t:t + 1], ALU.add, ALU.max, maxima[:, m:m + 1]
                                               ).then_inc(bank_free, 1)
                if first and m == 1 and 2 <= t + 1 < TILES:
                    add_bias(nc.vector, 2 * t + 3)
                if m < CHUNKS - 1:
                    return
                dve.wait_ge(bank_free, bank_no(h, s) + RING)
                nc.vector.tensor_reduce(top[:, :], maxima[:, :], AX.X, ALU.max).then_inc(bias_used, 1)
                dve.wait_ge(bias_used, h * TILES + (t + 1 + BIAS))
                nc.vector.tensor_scalar(shift[:, i:i + 1], top[:, :], -2.0, None, ALU.mult).then_inc(shift_ready, 1)
                if first and t + 2 < TILES:
                    write_masks(t + 2)
                if i == GROUP - 1:
                    dve.wait_ge(shift_ready, h * TILES + GROUP * (g + 1))
                    nc.vector.tensor_scalar(masked_arg[:, :], shift[:, :], MASKED, 0.0, ALU.add, ALU.min
                                            ).then_inc(masked_arg_ready, 1)

            def invert_denominators(h, first, g):
                tiles = slice(GROUP * g, GROUP * (g + 1))
                if first:
                    own(nc.vector.tensor_tensor(masked[:, tiles], masked_sum[:, tiles, 0], masked_sum[:, tiles, 1],
                                                ALU.add))
                    own(nc.vector.tensor_scalar(masked[:, tiles], masked[:, tiles], 1.0 / BIG, None, ALU.mult))
                dve.wait_ge(masked_exp_ready, h * GROUPS + g + 1)
                nc.vector.tensor_tensor(masked_part[:, :], masked[:, tiles], masked_exp[:, :], ALU.mult
                                        ).then_inc(step, 1)
                dve.wait_ge(step, h * STEPS + g * GROUP_STEPS + 1)
                dve.wait_ge(exp_ready, h * TILES + GROUP * (g + 1))
                nc.vector.tensor_tensor(denom[:, :], masked_part[:, :], exp_sum[:, :], ALU.add).then_inc(step, 1)
                dve.wait_ge(step, h * STEPS + g * GROUP_STEPS + 2)
                nc.vector.reciprocal(inv_denom[:, :], denom[:, :]).then_inc(step, 1)

            def add_output(h, s):
                g, b = s[1:]
                dve.wait_ge(step, h * STEPS + (g + 1) * GROUP_STEPS)
                dve.wait_ge(bank_full, bank_no(h, s))
                for n in range(2):
                    i = 2 * b + n
                    rows = y[:, GROUP * g + i, :]
                    last = nc.vector.scalar_tensor_tensor(
                        out=rows, in0=two(bank_of(h, s))[:, n, :], scalar=inv_denom[:, i:i + 1], in1=rows,
                        op0=ALU.mult, op1=ALU.add)
                last.then_inc(bank_free, 1)

            def split_output(h, g):
                for dc in range(KC):
                    dve.wait_ge(ot_hi_ready, h * (GROUPS * KC) + g * KC + dc + 1)
                    nc.vector.scalar_tensor_tensor(out=ot[:, 1, dc, :], in0=ot_acc[:, dc, :], scalar=1.0,
                                                   in1=ot[:, 0, dc, :].bitcast(F32), op0=ALU.mult,
                                                   op1=ALU.subtract).then_inc(ot_ready, 1)

            def head(h, first):
                for s in HEAD:
                    if s[0] in HALVED:
                        lo_part(h, s)
                    elif s[0] == "score":
                        bias_scores(h, first, s)
                    elif s[0] == "out":
                        add_output(h, s)
                    elif s[0] == "weigh" and s[2] == TILES - 1:
                        invert_denominators(h, first, s[1])
                        split_output(h, s[1])

            dve.sem_inc(bank_free, RING)
            dve.sem_inc(bias_used, BIAS)
            for n, s in enumerate(START):
                lo_part(None, s)
                if n in (3, 6):
                    write_masks(n // 3 - 1)
                if n in (5, 8):
                    for k in (0, 1):
                        add_bias(nc.vector, n // 3 * 2 - 2 + k)
            dve.wait_ge(y_loaded, 16 * BLOCKS)
            head(0, True)
            with dve.Fori(1, HEADS) as h:
                head(h, False)

            done = HEADS * STEPS
            dve.wait_ge(bank_free, HEADS * BANKS + START_BANKS + RING)
            for t in range(TILES):
                nc.vector.bn_stats(stats[:, t, :], y[:, t, :]).then_inc(step, 1)
            for t in range(TILES):
                dve.wait_ge(step, done + t + 1)
                nc.vector.bn_aggr(moments[:, t, :], stats[:, t, :]).then_inc(step, 1)
            dve.wait_ge(step, done + 2 * TILES)
            nc.vector.tensor_scalar(var_eps[:, :], moments[:, :, 1], EPS, None, ALU.add).then_inc(var_ready, 1)
            dve.wait_ge(std_ready, 1)
            nc.vector.reciprocal(inv_std[:, :], std[:, :]).then_inc(step, 1)
            dve.wait_ge(step, done + 2 * TILES + 1)
            for t in range(TILES):
                last = nc.vector.tensor_scalar(y[:, t, :], y[:, t, :], moments[:, t, 0:1], inv_std[:, t:t + 1],
                                               ALU.subtract, ALU.mult)
                if t % 2:
                    last.then_inc(out_ready, 1)


def kernel(x, adj, L0_gnn_Wq, L0_gnn_Wk, L0_gnn_Wv, L0_gnn_Wout):
    import concourse.bacc as bacc
    from concourse.bass_utils import run_bass_kernel_spmd

    nc = bacc.Bacc("TRN2", target_bir_lowering=False, num_devices=1)
    arrays = {"x": x, "adj": adj, "wq": L0_gnn_Wq, "wk": L0_gnn_Wk, "wv": L0_gnn_Wv, "wout": L0_gnn_Wout}
    arrays = {name: np.ascontiguousarray(a) for name, a in arrays.items()}
    aps = [nc.dram_tensor(name, a.shape, mybir.dt.from_np(a.dtype), kind="ExternalInput").ap()
           for name, a in arrays.items()]
    out = nc.dram_tensor("out", (N, HIDDEN), F32, kind="ExternalOutput").ap()
    build(nc, *aps, out)
    return run_bass_kernel_spmd(nc, [arrays], core_ids=[0]).results[0]["out"]
```

```python
from contextlib import ExitStack

import numpy as np
import concourse.bass as bass
from concourse import mybir

ALU = mybir.AluOpType
ACT = mybir.ActivationFunctionType
AX = mybir.AxisListType
F32 = mybir.dt.float32
F32R = mybir.dt.float32r
BF16 = mybir.dt.bfloat16

P = 128
HIDDEN = 256
HEADS = 8
N = 2048
ROWS = N // HEADS
BLOCKS = N // ROWS
KC = HIDDEN // P
TILES = N // P
GROUP = 4
GROUPS = TILES // GROUP
GN = GROUP * P
BANK = 512
CHUNKS = N // BANK
HALF = N // 2
HJ = HALF // BLOCKS

EPS = 1e-5
MASKED = -1.0e6
BIG = -(2.0 ** 100)
NONE = -1.0e38
Q_SCALE = HIDDEN ** -0.5 / 2

UNITS = ([("v", c) for c in range(BLOCKS)] + [("q", c) for c in range(2, BLOCKS)]
         + [("q", c) for c in range(2)] + [("k", c) for c in range(BLOCKS)])
NU = len(UNITS)
AHEAD = list(range(NU - BLOCKS - 2, NU))

RING = 6
RAW = 3
SPLIT = 2
BIAS = 4
PT = 3
MASKS = 4
NORMED = (range(TILES - GROUP), range(TILES - GROUP, TILES))


def schedule():
    units = iter(range(NU))

    def unit():
        return ("unit", next(units))

    steps = []
    for g in range(GROUPS):
        for n in range(GROUP * CHUNKS):
            steps.append(("score", g, n // CHUNKS, n % CHUNKS))
            if g == 0 and n in VALUES_AFTER:
                steps.append(unit())
        steps += [unit(), unit(), ("turn", g, 0), ("out", g - 1, 0), ("turn", g, 1), ("out", g - 1, 1)]
        for j in range(TILES):
            steps += [("turn", g, j + PT - 1)] if j + PT - 1 < TILES else []
            steps += [("wout",)] if g == j == 0 else []
            steps.append(("weigh", g, j))
            if g == GROUPS - 1 and j % 2 == 0:
                steps.append(unit())
        if g == GROUPS - 2:
            steps += [("x", kc) for kc in range(KC)]
    return steps


VALUES_AFTER = (1, 2, 4, 6, 8, 10, 12, 14)
HEAD = schedule()
START = [("x", kc) for kc in range(KC)] + [("unit", k) for k in AHEAD]
FIRST = [s for s in HEAD if s[:2] != ("out", -1)]
END = [("out", -1, b) for b in range(2)]
HANDED = ("score", "unit", "x", "out", "turn")
HALVED = ("unit", "x", "turn")


def bias_schedule():
    start, work = {}, {}

    def do(where, s, *what):
        where.setdefault(s, []).append(what)

    for half in range(2):
        for n, what in ((3, "mask"), (4, "count"), (7, "add")):
            do(start, START[n + 2 * half], what, 0, half)
        do(work, ("score", 0, 0, half), "mask", 1, half)
        do(work, ("score", 0, 0, half), "count", 1, half)
        do(work, ("score", 0, 0, 2 + half), "add", 1, half)
        do(work, ("score", 0, 0, 2 + half), "mask", 2, half)
        do(work, ("score", 0, 0, 2 + half), "count", 2, half)
        do(work, ("score", 0, 1, 2 * half), "mask", 3, half)
        do(work, ("score", 0, 1, 2 * half), "count", 3, half)
    do(work, ("score", 0, 0, 3), "pass", 1)
    for g in range(GROUPS):
        for i in range(2):
            t = GROUP * g + i + 2
            do(work, ("score", g, i, CHUNKS - 1), "add", t, 0)
            do(work, ("score", g, i + 1, 1), "add", t, 1)
            do(work, ("score", g, i + 1, 1), "pass", t)
        if g:
            for half in range(2):
                do(work, ("score", g, 0, half), "mask", GROUP * g + 3, half)
                do(work, ("score", g, 0, half), "count", GROUP * g + 3, half)
        if g < GROUPS - 1:
            for i in range(2):
                t, j = GROUP * (g + 1) + i, 5 * i + 3
                for half in range(2):
                    do(work, ("turn", g, j + 2 * half), "mask", t, half)
                    do(work, ("turn", g, j + 2 * half), "count", t, half)
                    do(work, ("turn", g, j + 2 + 2 * half), "add", t, half)
                do(work, ("turn", g, j + 4), "pass", t)
            for half in range(2):
                do(work, ("turn", g, TILES - 3 + 2 * half), "mask", GROUP * (g + 1) + 2, half)
                do(work, ("turn", g, TILES - 3 + 2 * half), "count", GROUP * (g + 1) + 2, half)
    return start, work


def numbers(steps, kinds):
    return {s: n for n, s in enumerate([s for s in steps if s[0] in kinds])}


BANK_NO, START_BANK_NO, FIRST_BANK_NO = (numbers(steps, HANDED) for steps in (HEAD, START, FIRST))
HI_NO, START_HI_NO = numbers(HEAD, HALVED), numbers(START, HALVED)
BANKS, START_BANKS, FIRST_BANKS = len(BANK_NO), len(START_BANK_NO), len(FIRST_BANK_NO)
BEFORE_LOOP = START_BANKS + FIRST_BANKS
HIS, START_HIS = len(HI_NO), len(START_HI_NO)
START_UNITS = len(AHEAD)
START_BIAS, FIRST_BIAS = bias_schedule()
assert BANKS % RING == 0 and NU % RAW == 0 and NU % SPLIT == 0


def build(nc, x, adj, wq, wk, wv, wout, out):
    adj_rows = adj.rearrange("(s p c) m -> c s p m", p=P, c=BLOCKS)
    x_rows = x.rearrange("(s p c) d -> c p s d", p=P, c=BLOCKS)
    out_rows = out.rearrange("(s p c) d -> c p s d", p=P, c=BLOCKS)
    weights = {"q": wq, "k": wk, "v": wv}
    bias_kept = nc.dram_tensor("bias_kept", (TILES, P, N), F32, kind="Internal").ap()

    with ExitStack() as ctx:
        def sb(name, shape, dt=F32):
            return ctx.enter_context(nc.sbuf_tensor(name, shape, dt))

        def sem(name):
            return ctx.enter_context(nc.semaphore(name))

        kt = sb("kt", [P, 2, KC, N], F32R)
        vv = sb("vv", [P, 2, TILES, HIDDEN], F32R)
        qt = sb("qt", [P, 2, KC, GN], F32R)
        xt = sb("xt", [P, 2, KC, ROWS], F32R)
        pt = sb("pt", [P, PT, 2, GN], F32R)
        ot = sb("ot", [P, 2, KC, GN], F32R)
        w_split = sb("w_split", [P, SPLIT, 2, KC, HIDDEN], F32R)
        wout_split = sb("wout_split", [P, 2, KC, HIDDEN], F32R)
        w_raw = sb("w_raw", [P, RAW, KC, HIDDEN])
        wout_raw = sb("wout_raw", [P, KC, HIDDEN])
        x_raw = sb("x_raw", [P, ROWS // P, HIDDEN])
        bias = sb("bias", [P, BIAS, N])
        mask = sb("mask", [P, MASKS, HALF], BF16)
        probs = sb("probs", [P, GROUP, N])
        y = sb("y", [P, TILES, HIDDEN])
        ident = sb("ident", [P, P])
        maxima = sb("maxima", [P, CHUNKS])
        top = sb("top", [P, 1])
        shift = sb("shift", [P, GROUP])
        masked_sum = sb("masked_sum", [P, TILES, 2])
        unmasked = sb("unmasked", [P, 1])
        floor = sb("floor", [P, TILES])
        masked = sb("masked", [P, TILES])
        exp_sum = sb("exp_sum", [P, GROUP + 1])
        masked_arg = sb("masked_arg", [P, GROUP])
        masked_exp = sb("masked_exp", [P, GROUP])
        masked_part = sb("masked_part", [P, GROUP])
        denom = sb("denom", [P, GROUP])
        inv_denom = sb("inv_denom", [P, GROUP])
        stats = sb("stats", [P, TILES, 6])
        moments = sb("moments", [P, TILES, 2])
        var_eps = sb("var_eps", [P, TILES])
        std = sb("std", [P, TILES])
        inv_std = sb("inv_std", [P, TILES])

        ring = ctx.enter_context(nc.psum_tensor("ring", [P, RING, BANK], F32))
        ot_acc = ctx.enter_context(nc.psum_tensor("ot_acc", [P, KC, BANK], F32))

        y_loaded = sem("y_loaded")
        x_loaded = sem("x_loaded")
        wout_loaded = sem("wout_loaded")
        wout_hi_ready = sem("wout_hi_ready")
        wout_ready = sem("wout_ready")
        w_loaded = [sem(f"w_loaded{s}") for s in range(RAW)]
        start_loaded = [sem(f"start_loaded{n}") for n in range(START_UNITS)]
        w_hi_ready = sem("w_hi_ready")
        w_ready = sem("w_ready")
        adj_loaded = [sem(f"adj_loaded{s}") for s in range(4)]
        mask_ready = sem("mask_ready")
        mask_counted = sem("mask_counted")
        bias_ready = {"pool": sem("bias_ready_pool"), "dve": sem("bias_ready_dve")}
        bias_stored = [sem(f"bias_stored{s}") for s in range(2)]
        bias_loaded = [sem(f"bias_loaded{s}") for s in range(BIAS)]
        bias_used = sem("bias_used")
        ident_ready = sem("ident_ready")
        bank_full = sem("bank_full")
        bank_free = sem("bank_free")
        hi_ready = sem("hi_ready")
        shift_ready = sem("shift_ready")
        exp_ready = sem("exp_ready")
        masked_arg_ready = sem("masked_arg_ready")
        masked_exp_ready = sem("masked_exp_ready")
        ot_full = sem("ot_full")
        ot_hi_ready = sem("ot_hi_ready")
        ot_ready = sem("ot_ready")
        step = sem("step")
        first_step = sem("first_step")
        pool_step = sem("pool_step")
        dve_gate = sem("dve_gate")
        var_ready = sem("var_ready")
        std_ready = sem("std_ready")
        out_ready = sem("out_ready")
        stored = sem("stored")

        def is_first(h):
            return isinstance(h, int) and h == 0

        def is_end(h):
            return isinstance(h, int) and h == HEADS

        def bank_no(h, s):
            if h is None:
                return START_BANK_NO[s] + 1
            if is_first(h):
                return START_BANKS + FIRST_BANK_NO[s] + 1
            if is_end(h):
                return (HEADS - 1) * BANKS + BEFORE_LOOP + END.index(s) + 1
            return h * BANKS + (BEFORE_LOOP - BANKS + BANK_NO[s] + 1)

        def hi_no(h, s):
            return START_HI_NO[s] + 1 if h is None else h * HIS + (START_HIS + HI_NO[s] + 1)

        def unit_no(h, k):
            return AHEAD.index(k) + 1 if h is None else h * NU + (START_UNITS + k + 1)

        def unit_raw(h, k):
            if h is None:
                i, n = divmod(AHEAD.index(k), CHUNKS)
                return probs[:, i, n * BANK:(n + 1) * BANK].rearrange("p (k n) -> p k n", k=KC)
            return w_raw[:, k % RAW, :, :]

        def unit_split(h, k):
            if h is None:
                n = AHEAD.index(k) % BLOCKS
                return vv[:, :, KC * n:KC * (n + 1), :]
            return w_split[:, k % SPLIT, :, :, :]

        def unit_loaded(h, k):
            if h is None:
                return start_loaded[AHEAD.index(k)], 16
            return w_loaded[k % RAW], h * (NU // RAW * 16) + (k // RAW + 1) * 16

        def bank_of(h, s):
            if h is None or is_first(h) or is_end(h):
                return ring[:, (bank_no(h, s) - 1) % RING, :]
            return ring[:, (BEFORE_LOOP + BANK_NO[s]) % RING, :]

        def two(ap):
            return ap.rearrange("p (a b) -> p a b", a=2)

        def split_of(h, s):
            if s[0] == "x":
                return [xt[:, part, s[1], :] for part in range(2)], bank_of(h, s)[:, 0:ROWS], 1.0
            if s[0] == "turn":
                return [pt[:, s[2] % PT, part, :] for part in range(2)], bank_of(h, s), 1.0
            kind, c = UNITS[s[1]]
            if kind == "k":
                dst = [kt[:, part, :, c * ROWS:(c + 1) * ROWS] for part in range(2)]
            elif kind == "v":
                dst = [vv[:, part, 2 * c:2 * c + 2, :] for part in range(2)]
            else:
                dst = [qt[:, part, :, c % 2 * ROWS:(c % 2 + 1) * ROWS] for part in range(2)]
            return dst, two(bank_of(h, s)), Q_SCALE if kind == "q" else 1.0

        EXPS = GROUP + 1

        def tile_ends(s):
            return s[0] == "score" and s[3] == CHUNKS - 1

        def bias_slot(first, t):
            return bias[:, t % 2 if first else t % BIAS, :]

        def adj_slot(k):
            return bias[:, 2 + k % 4 // 2, k % 2 * HALF:(k % 2 + 1) * HALF]

        def maker(k):
            return "dve" if k % 2 or k < 4 else "pool"

        def wait_for_bias(eng, k):
            eng.wait_ge(bias_ready[maker(k)], sum(maker(n) == maker(k) for n in range(k + 1)))

        def add_bias(eng, k):
            t = k // 2
            eng.wait_ge(mask_counted, k + 1)
            if t >= 2:
                eng.wait_ge(bias_used, BIAS + t - 1)
                eng.wait_ge(bias_stored[t % 2], 16 * (t // 2))
            dst = bias_slot(True, t).rearrange("p (c i) -> p c i", c=BLOCKS)
            eng.tensor_tensor(dst[:, :, k % 2 * HJ:(k % 2 + 1) * HJ],
                              adj_slot(k).rearrange("p (i c) -> p c i", c=BLOCKS),
                              mask[:, k % MASKS, :].rearrange("p (i c) -> p c i", c=BLOCKS),
                              ALU.add).then_inc(bias_ready[maker(k)], 1)

        block = ctx.enter_context(nc.Block())

        @block.sync
        def _(sp):
            def load_x(first_row):
                sp.dma_start(x_raw[:, :, :], x[bass.ds(first_row, ROWS), :].rearrange(
                    "(s p) d -> p s d", p=P)).then_inc(x_loaded, 16)

            def load_unit(h, k):
                kind, c = UNITS[k]
                if h is not None and not (is_first(h) and k < RAW):
                    sp.wait_ge(w_ready, unit_no(h, k))
                sp.dma_start(unit_raw(h, k), weights[kind].rearrange(
                    "(k p) n -> p k n", p=P)[:, :, c * HIDDEN:(c + 1) * HIDDEN]
                             ).then_inc(unit_loaded(h, k)[0], 16)

            def load_adj(k):
                if k >= 4:
                    wait_for_bias(sp, k - 4)
                sp.dma_start(adj_slot(k), adj_rows[k // 4, k // 2 % 2, :, k % 2 * HALF:(k % 2 + 1) * HALF]
                             ).then_inc(adj_loaded[k % 4], 16)

            def store_bias(t):
                for k in (2 * t, 2 * t + 1):
                    wait_for_bias(sp, k)
                sp.dma_start(bias_kept[t], bias_slot(True, t)).then_inc(bias_stored[t % 2], 16)

            def pass_bias(t):
                if t + 2 < TILES:
                    load_adj(2 * t + 4)
                    load_adj(2 * t + 5)
                store_bias(t)

            def load_bias(h, t):
                sp.wait_ge(bias_used, h * TILES + t + 1)
                sp.dma_start(bias_slot(False, t), bias_kept[t]).then_inc(bias_loaded[t % BIAS], 16)

            def begin(h):
                sp.wait_ge(bank_full, bank_no(None if is_first(h) else h - 1, ("x", KC - 1)))
                load_x(((h + 1) % HEADS) * ROWS)
                sp.wait_ge(wout_ready, h + 1)
                sp.dma_start(wout_raw[:, :, :], wout[bass.ds(h * HIDDEN, HIDDEN), :].rearrange(
                    "(k p) n -> p k n", p=P)).then_inc(wout_loaded, 16)

            def feed(h, s, first=False):
                if s[0] == "unit" and s[1] + RAW + SPLIT < NU:
                    load_unit(h, s[1] + RAW + SPLIT)
                if first:
                    for kind, t, *_ in FIRST_BIAS.get(s, ()):
                        if kind == "pass":
                            pass_bias(t)
                elif tile_ends(s) and GROUP * s[1] + s[2] + BIAS < TILES:
                    load_bias(h, GROUP * s[1] + s[2] + BIAS)

            last_scores = HEAD.index(("score", GROUPS - 1, GROUP - 1, CHUNKS - 1))
            before, behind = HEAD[:last_scores + 1], HEAD[last_scores + 1:]

            load_x(0)
            for n, k in enumerate(AHEAD):
                load_unit(None, k)
                if n in (1, 2, 3, 4):
                    load_adj(n - 1)
            for k in range(RAW + SPLIT):
                load_unit(0, k)
            pass_bias(0)
            begin(0)
            for s in before:
                feed(0, s, True)
                if s == ("score", 0, GROUP - 1, CHUNKS - 1):
                    for c in range(BLOCKS):
                        sp.dma_start(y[:, 2 * c:2 * c + 2, :], x_rows[c]).then_inc(y_loaded, 16)
            for s in range(2):
                sp.wait_ge(bias_stored[s], 16 * (TILES // 2))
            sp.wait_ge(bias_used, BIAS + TILES)
            with sp.Fori(1, HEADS) as h:
                coming = iter(range(BIAS))
                for s in behind:
                    feed(h - 1, s)
                    if s[0] == "turn" and s[2] < BIAS:
                        load_bias(h, next(coming))
                for k in range(RAW + SPLIT):
                    load_unit(h, k)
                begin(h)
                for s in before:
                    feed(h, s)
            for s in behind:
                feed(HEADS - 1, s)
            for c in range(BLOCKS):
                sp.wait_ge(out_ready, c + 1)
                sp.dma_start(out_rows[c], y[:, 2 * c:2 * c + 2, :]).then_inc(stored, 16)
            sp.wait_ge(stored, 16 * BLOCKS)

        @block.gpsimd
        def _(pool):
            def lo_unit(h, k):
                split = unit_split(h, k)
                pool.wait_ge(w_hi_ready, unit_no(h, k))
                nc.gpsimd.tensor_tensor(split[:, 1], unit_raw(h, k), split[:, 0].bitcast(F32), ALU.subtract
                                        ).then_inc(w_ready, 1)

            def head(h, first):
                for k in range(SPLIT):
                    lo_unit(h, k)
                for s in HEAD:
                    if s[0] == "unit" and s[1] + SPLIT < NU:
                        lo_unit(h, s[1] + SPLIT)
                    elif s[0] == "wout":
                        pool.wait_ge(wout_hi_ready, h + 1)
                        nc.gpsimd.tensor_tensor(wout_split[:, 1, :, :], wout_raw[:, :, :],
                                                wout_split[:, 0, :, :].bitcast(F32), ALU.subtract
                                                ).then_inc(wout_ready, 1)
                    if first:
                        for kind, t, *half in FIRST_BIAS.get(s, ()):
                            if kind == "add" and maker(2 * t + half[0]) == "pool":
                                add_bias(nc.gpsimd, 2 * t + half[0])

            nc.gpsimd.memset(ident[:, :], 0.0).then_inc(pool_step, 1)
            pool.wait_ge(pool_step, 1)
            nc.gpsimd.affine_select(out=ident[:, :], in_=ident[:, :], compare_op=ALU.not_equal, fill=1.0, base=0,
                                    pattern=[[-1, P]], channel_multiplier=1).then_inc(ident_ready, 1)
            pool.sem_inc(w_ready, RAW)
            pool.sem_inc(wout_ready, 1)
            for k in AHEAD:
                lo_unit(None, k)
            head(0, True)
            with pool.Fori(1, HEADS) as h:
                head(h, False)

        @block.scalar
        def _(act):
            def hi_unit(h, k):
                act.wait_ge(*unit_loaded(h, k))
                nc.scalar.activation(unit_split(h, k)[:, 0], unit_raw(h, k), ACT.Copy).then_inc(w_hi_ready, 1)

            def hi_part(h, s):
                dst, src, factor = split_of(h, s)
                act.wait_ge(bank_full, bank_no(h, s))
                nc.scalar.activation(dst[0], src, ACT.Copy, scale=factor).then_inc(hi_ready, 1)

            def before_turn(n):
                return any(s[0] == "turn" and s[2] == 0 for s in HEAD[n + 1:n + 3])

            def count(work):
                for kind, t, *half in work:
                    if kind == "count":
                        k = 2 * t + half[0]
                        act.wait_ge(mask_ready, k + 1)
                        nc.scalar.activation(mask[:, k % MASKS, :], mask[:, k % MASKS, :], ACT.Copy,
                                             accum_out=masked_sum[:, t, k % 2:k % 2 + 1]).then_inc(mask_counted, 1)

            def head(h, first):
                for k in range(SPLIT):
                    hi_unit(h, k)
                put_off = []
                for n, s in enumerate(HEAD):
                    if s[0] == "unit" and s[1] + SPLIT < NU:
                        if before_turn(n):
                            put_off.append(s[1] + SPLIT)
                        else:
                            act.wait_ge(bank_full, bank_no(h, s))
                            hi_unit(h, s[1] + SPLIT)
                    if s[0] in HALVED:
                        hi_part(h, s)
                    if s[0] == "turn" and s[2] == 1:
                        for k in put_off:
                            hi_unit(h, k)
                        put_off = []
                    elif s[0] == "wout":
                        act.wait_ge(wout_loaded, h * 16 + 16)
                        nc.scalar.activation(wout_split[:, 0, :, :], wout_raw[:, :, :], ACT.Copy
                                             ).then_inc(wout_hi_ready, 1)
                    elif tile_ends(s):
                        g, i = s[1], s[2]
                        t = GROUP * g + i
                        act.wait_ge(shift_ready, h * TILES + t + 1)
                        for cut in [slice(0, N)] if i < GROUP - 1 else [slice(0, HALF), slice(HALF, N)]:
                            n = i + (cut.start > 0)
                            nc.scalar.activation(probs[:, i, cut], probs[:, i, cut], ACT.Exp, bias=shift[:, i:i + 1],
                                                 scale=2.0, accum_out=exp_sum[:, n:n + 1]).then_inc(exp_ready, 1)
                        if i == GROUP - 1:
                            act.wait_ge(masked_arg_ready, h * GROUPS + g + 1)
                            nc.scalar.activation(masked_exp[:, :], masked_arg[:, :], ACT.Exp
                                                 ).then_inc(masked_exp_ready, 1)
                    elif s[0] == "weigh" and s[2] == TILES - 1:
                        for dc in range(KC):
                            act.wait_ge(ot_full, h * (GROUPS * KC) + s[1] * KC + dc + 1)
                            nc.scalar.activation(ot[:, 0, dc, :], ot_acc[:, dc, :], ACT.Copy
                                                 ).then_inc(ot_hi_ready, 1)
                    if first:
                        count(FIRST_BIAS.get(s, ()))

            units = iter(AHEAD)
            hi_unit(None, next(units))
            for s in START:
                hi_part(None, s)
                for k in (next(units, None),):
                    if k is not None:
                        hi_unit(None, k)
                count(START_BIAS.get(s, ()))
            head(0, True)
            with act.Fori(1, HEADS) as h:
                head(h, False)
            for part, tiles in enumerate(NORMED):
                cut = slice(tiles[0], tiles[-1] + 1)
                act.wait_ge(var_ready, part + 1)
                nc.scalar.activation(std[:, cut], var_eps[:, cut], ACT.Sqrt).then_inc(std_ready, 1)

        @block.tensor
        def _(pe):
            def product(dst, lhs, rhs, first, last):
                nc.tensor.matmul(dst, lhs(1), rhs(0), start=first, stop=False)
                nc.tensor.matmul(dst, lhs(0), rhs(1), start=False, stop=False)
                return nc.tensor.matmul(dst, lhs(0), rhs(0), start=False, stop=last)

            def turn_x(bank, kc):
                for n in range(ROWS // P):
                    last = nc.tensor.transpose(bank[:, n * P:(n + 1) * P], x_raw[:, n, kc * P:(kc + 1) * P],
                                               ident[:, :])
                return last

            def project(h, bank, k):
                pe.wait_ge(w_ready, unit_no(h, k) + RAW)
                w = unit_split(h, k)
                for b in range(2):
                    cut = slice(b * P, (b + 1) * P)
                    for kc in range(KC):
                        def of_x(part, cols=slice(0, ROWS)):
                            return xt[:, part, kc, cols]

                        def of_w(part, cols=slice(0, HIDDEN)):
                            return w[:, part, kc, cols]

                        if UNITS[k][0] == "v":
                            last = product(two(bank)[:, b, :], lambda n: of_x(n, cut), of_w, kc == 0, kc == KC - 1)
                        else:
                            last = product(two(bank)[:, b, :], lambda n: of_w(n, cut), of_x, kc == 0, kc == KC - 1)
                return last

            def score(h, first, bank, g, i, m):
                if g and i == m == 0:
                    pe.wait_ge(bank_free, bank_no(h, ("unit", UNITS.index(("q", 2 * g + 1)))) + RING)
                if not g and not i:
                    keys = UNITS.index(("k", (m + 1) * BANK // ROWS - 1))
                    pe.wait_ge(bank_free, bank_no(None if first else h - 1, ("unit", keys)) + RING)
                for dc in range(KC):
                    last = product(bank, lambda n: qt[:, n, dc, i * P:(i + 1) * P],
                                   lambda n: kt[:, n, dc, m * BANK:(m + 1) * BANK], dc == 0, dc == KC - 1)
                return last

            def out_product(h, bank, g, b):
                if b == 0:
                    pe.wait_ge(ot_ready, h * (GROUPS * KC) + (g + 1) * KC)
                    pe.wait_ge(wout_ready, h + (2 if g >= 0 else 1))
                for n in range(2):
                    cut = slice((2 * b + n) * P, (2 * b + n + 1) * P)
                    for dc in range(KC):
                        last = product(two(bank)[:, n, :], lambda part: ot[:, part, dc, cut],
                                       lambda part: wout_split[:, part, dc, :], dc == 0, dc == KC - 1)
                return last

            def turn_probs(h, bank, g, j):
                for i in range(GROUP):
                    if j == 0 or (j == TILES // 2 and i == GROUP - 1):
                        pe.wait_ge(exp_ready, h * (GROUPS * EXPS) + (EXPS * g + i + 1 + (j > 0)))
                    last = nc.tensor.transpose(bank[:, i * P:(i + 1) * P], probs[:, i, j * P:(j + 1) * P],
                                               ident[:, :])
                return last

            def weigh(h, g, j):
                pe.wait_ge(bank_free, bank_no(h, ("turn", g, j)) + RING)
                for dc in range(KC):
                    last = product(ot_acc[:, dc, :], lambda n: vv[:, n, j, dc * P:(dc + 1) * P],
                                   lambda n: pt[:, j % PT, n, :], j == 0, j == TILES - 1)
                    if j == TILES - 1:
                        last.then_inc(ot_full, 1)

            def run(h, steps, first=True):
                for s in steps:
                    if s[0] in HANDED:
                        bank = bank_of(h, s)
                        pe.wait_ge(bank_free, bank_no(h, s))
                    if s[0] == "x":
                        if s[1] == 0:
                            pe.wait_ge(x_loaded, 16 if h is None else h * 16 + 32)
                        turn_x(bank, s[1]).then_inc(bank_full, 1)
                    elif s[0] == "unit":
                        if s[1] == AHEAD[0]:
                            pe.wait_ge(bank_free, bank_no(h, ("x", KC - 1)) + RING)
                        project(h, bank, s[1]).then_inc(bank_full, 1)
                    elif s[0] == "score":
                        score(h, first, bank, *s[1:]).then_inc(bank_full, 1)
                    elif s[0] == "out":
                        out_product(h, bank, *s[1:]).then_inc(bank_full, 1)
                    elif s[0] == "turn":
                        turn_probs(h, bank, *s[1:]).then_inc(bank_full, 1)
                    elif s[0] == "weigh":
                        weigh(h, *s[1:])

            pe.wait_ge(ident_ready, 1)
            run(None, START)
            run(0, FIRST)
            with pe.Fori(1, HEADS) as h:
                run(h, HEAD, False)
            run(HEADS, END)

        @block.vector
        def _(dve):
            GROUP_STEPS = 4
            STEPS = GROUPS * GROUP_STEPS
            made = [0]

            def own(ins):
                made[0] += 1
                ins.then_inc(first_step, 1)
                dve.wait_ge(first_step, made[0])

            def lo_part(h, s):
                dst, src, factor = split_of(h, s)
                dve.wait_ge(hi_ready, hi_no(h, s))
                nc.vector.scalar_tensor_tensor(out=dst[1], in0=src, scalar=factor, in1=dst[0].bitcast(F32),
                                               op0=ALU.mult, op1=ALU.subtract).then_inc(bank_free, 1)

            def make_bias(work):
                for kind, t, *half in work:
                    if kind in ("pass", "count"):
                        continue
                    k = 2 * t + half[0]
                    if kind == "mask":
                        dve.wait_ge(adj_loaded[k % 4], (k // 4 + 1) * 16)
                        if k >= MASKS:
                            wait_for_bias(dve, k - MASKS)
                        nc.vector.tensor_scalar(mask[:, k % MASKS, :], adj_slot(k), 0.0, BIG, ALU.is_equal,
                                                ALU.mult).then_inc(mask_ready, 1)
                    elif maker(k) == "dve":
                        add_bias(nc.vector, k)

            def find_floor(t):
                dve.wait_ge(mask_counted, 2 * t + 2)
                own(nc.vector.tensor_scalar(unmasked[:, :], masked_sum[:, t, 0:1], masked_sum[:, t, 1:2], 0.0,
                                            ALU.add, ALU.is_equal))
                own(nc.vector.tensor_scalar(floor[:, t:t + 1], unmasked[:, :], NONE, MASKED / 2, ALU.mult, ALU.min))

            def bias_scores(h, first, s):
                g, i, m = s[1:]
                t = GROUP * g + i
                if m == 0:
                    if first:
                        find_floor(t)
                        for k in (2 * t, 2 * t + 1):
                            wait_for_bias(dve, k)
                    else:
                        dve.wait_ge(bias_loaded[t % BIAS], h * (TILES // BIAS * 16)
                                    + (t // BIAS + 1 - TILES // BIAS) * 16)
                dve.wait_ge(bank_full, bank_no(h, s))
                dve.sem_inc(dve_gate, 1)
                cut = slice(m * BANK, (m + 1) * BANK)
                nc.vector.tensor_tensor_reduce(probs[:, i, cut], bank_of(h, s), bias_slot(first, t)[:, cut],
                                               1.0, floor[:, t:t + 1], ALU.add, ALU.max, maxima[:, m:m + 1]
                                               ).then_inc(bank_free, 1)
                if m < CHUNKS - 1:
                    return
                dve.wait_ge(bank_free, bank_no(h, s) + RING)
                nc.vector.tensor_reduce(top[:, :], maxima[:, :], AX.X, ALU.max).then_inc(bias_used, 1)
                dve.wait_ge(bias_used, h * TILES + (t + 1 + BIAS))
                nc.vector.tensor_scalar(shift[:, i:i + 1], top[:, :], -2.0, None, ALU.mult).then_inc(shift_ready, 1)
                if i == GROUP - 1:
                    dve.wait_ge(shift_ready, h * TILES + GROUP * (g + 1))
                    nc.vector.tensor_scalar(masked_arg[:, :], shift[:, :], MASKED, 0.0, ALU.add, ALU.min
                                            ).then_inc(masked_arg_ready, 1)

            def invert_denominators(h, first, g):
                tiles = slice(GROUP * g, GROUP * (g + 1))
                if first:
                    own(nc.vector.tensor_tensor(masked[:, tiles], masked_sum[:, tiles, 0], masked_sum[:, tiles, 1],
                                                ALU.add))
                    own(nc.vector.tensor_scalar(masked[:, tiles], masked[:, tiles], 1.0 / BIG, None, ALU.mult))
                dve.wait_ge(masked_exp_ready, h * GROUPS + g + 1)
                nc.vector.tensor_tensor(masked_part[:, :], masked[:, tiles], masked_exp[:, :], ALU.mult
                                        ).then_inc(step, 1)
                dve.wait_ge(step, h * STEPS + g * GROUP_STEPS + 1)
                dve.wait_ge(exp_ready, h * (GROUPS * EXPS) + EXPS * (g + 1))
                nc.vector.tensor_tensor(denom[:, :], masked_part[:, :], exp_sum[:, 0:GROUP], ALU.add
                                        ).then_inc(step, 1)
                dve.wait_ge(step, h * STEPS + (g * GROUP_STEPS + 2))
                nc.vector.tensor_tensor(denom[:, GROUP - 1:GROUP], denom[:, GROUP - 1:GROUP],
                                        exp_sum[:, GROUP:GROUP + 1], ALU.add).then_inc(step, 1)
                dve.wait_ge(step, h * STEPS + (g * GROUP_STEPS + 3))
                nc.vector.reciprocal(inv_denom[:, :], denom[:, :]).then_inc(step, 1)

            def add_output(h, s):
                g, b = s[1:]
                dve.wait_ge(step, h * STEPS + (g + 1) * GROUP_STEPS)
                dve.wait_ge(bank_full, bank_no(h, s))
                for n in range(2):
                    i = 2 * b + n
                    rows = y[:, GROUP * (g % GROUPS) + i, :]
                    last = nc.vector.scalar_tensor_tensor(
                        out=rows, in0=two(bank_of(h, s))[:, n, :], scalar=inv_denom[:, i:i + 1], in1=rows,
                        op0=ALU.mult, op1=ALU.add)
                last.then_inc(bank_free, 1)

            def split_output(h, g):
                for dc in range(KC):
                    dve.wait_ge(ot_hi_ready, h * (GROUPS * KC) + g * KC + dc + 1)
                    nc.vector.scalar_tensor_tensor(out=ot[:, 1, dc, :], in0=ot_acc[:, dc, :], scalar=1.0,
                                                   in1=ot[:, 0, dc, :].bitcast(F32), op0=ALU.mult,
                                                   op1=ALU.subtract).then_inc(ot_ready, 1)

            def head(h, first):
                for s in FIRST if first else HEAD:
                    if s[0] in HALVED:
                        lo_part(h, s)
                    elif s[0] == "score":
                        bias_scores(h, first, s)
                    elif s[0] == "out":
                        if first and s == ("out", 0, 0):
                            dve.wait_ge(y_loaded, 16 * BLOCKS)
                        add_output(h, s)
                    elif s[0] == "weigh" and s[2] == TILES - 1:
                        invert_denominators(h, first, s[1])
                        split_output(h, s[1])
                    if first:
                        make_bias(FIRST_BIAS.get(s, ()))

            dve.sem_inc(bank_free, RING)
            dve.sem_inc(bias_used, BIAS)
            for s in START:
                lo_part(None, s)
                make_bias(START_BIAS.get(s, ()))
            head(0, True)
            with dve.Fori(1, HEADS) as h:
                head(h, False)

            done = [HEADS * STEPS]

            def normed(ins):
                done[0] += 1
                ins.then_inc(step, 1)

            for part, tiles in enumerate(NORMED):
                if part:
                    for s in END:
                        add_output(HEADS, s)
                dve.wait_ge(bank_free, bank_no(HEADS, END[-1]) + RING if part
                            else bank_no(HEADS, END[0]) - 1 + RING)
                for t in tiles:
                    normed(nc.vector.bn_stats(stats[:, t, :], y[:, t, :]))
                dve.wait_ge(step, done[0])
                for t in tiles:
                    normed(nc.vector.bn_aggr(moments[:, t, :], stats[:, t, :]))
                dve.wait_ge(step, done[0])
                cut = slice(tiles[0], tiles[-1] + 1)
                nc.vector.tensor_scalar(var_eps[:, cut], moments[:, cut, 1], EPS, None, ALU.add
                                        ).then_inc(var_ready, 1)
            for part, tiles in enumerate(NORMED):
                cut = slice(tiles[0], tiles[-1] + 1)
                dve.wait_ge(std_ready, part + 1)
                normed(nc.vector.reciprocal(inv_std[:, cut], std[:, cut]))
                dve.wait_ge(step, done[0])
                for t in tiles:
                    last = nc.vector.tensor_scalar(y[:, t, :], y[:, t, :], moments[:, t, 0:1], inv_std[:, t:t + 1],
                                                   ALU.subtract, ALU.mult)
                    if t % 2:
                        last.then_inc(out_ready, 1)


def kernel(x, adj, L0_gnn_Wq, L0_gnn_Wk, L0_gnn_Wv, L0_gnn_Wout):
    import concourse.bacc as bacc
    from concourse.bass_utils import run_bass_kernel_spmd

    nc = bacc.Bacc("TRN2", target_bir_lowering=False, num_devices=1)
    arrays = {"x": x, "adj": adj, "wq": L0_gnn_Wq, "wk": L0_gnn_Wk, "wv": L0_gnn_Wv, "wout": L0_gnn_Wout}
    arrays = {name: np.ascontiguousarray(a) for name, a in arrays.items()}
    aps = [nc.dram_tensor(name, a.shape, mybir.dt.from_np(a.dtype), kind="ExternalInput").ap()
           for name, a in arrays.items()]
    out = nc.dram_tensor("out", (N, HIDDEN), F32, kind="ExternalOutput").ap()
    build(nc, *aps, out)
    return run_bass_kernel_spmd(nc, [arrays], core_ids=[0]).results[0]["out"]
```
